# Optimizing a Trainium2 kernel written in Bass

```python
import numpy as np
import jax
import jax.numpy as jnp

def _softmax(x, axis=-1):
    return jax.nn.softmax(x, axis=axis)

def _gelu(x):
    return jax.nn.gelu(x, approximate=True)

def _silu(x):
    return jax.nn.silu(x)

def _sigmoid(x):
    return jax.nn.sigmoid(x)

def _layernorm(x, axis=-1, eps=1e-05):
    m = jnp.mean(x, axis=axis, keepdims=True)
    v = jnp.var(x, axis=axis, keepdims=True)
    return (x - m) / jnp.sqrt(v + eps)

def _scatter_add(tgt, idx, src, axis=0):
    return tgt.at[idx].add(src)

def _segment_sum(src, seg, n):
    return jax.ops.segment_sum(src, seg, n)
kernel_name = 'mk_flamingo_gated_d1_seqx_r8_3e94d3'

def setup_inputs(seed: int=0):
    np.random.seed(seed)
    _w = jnp.asarray

    def _rec_inputs():
        import jax
        import jax.numpy as jnp
        _rk = jax.random.key(seed)
        x = -0.0003929 + 0.9999 * jax.random.normal(jax.random.fold_in(_rk, 1), (8, 128, 128), jnp.float32)
        _lenS = 128 - jax.random.randint(jax.random.fold_in(_rk, 7), (8,), 0, max(1, 128 // 4) + 1, jnp.int32)
        _lenS2 = 128 - jax.random.randint(jax.random.fold_in(_rk, 8), (8,), 0, max(1, 128 // 4) + 1, jnp.int32)
        _ctx_1024P = jax.random.normal(jax.random.fold_in(_rk, 11), (8, 16, 128), jnp.float32)
        _ctx_1024c = jax.random.dirichlet(jax.random.fold_in(_rk, 511), 0.3 * jnp.ones((16,), jnp.float32), (8, 128))
        _ctx_1024t = jnp.einsum('bsk,bkd->bsd', _ctx_1024c, _ctx_1024P)
        _ctx_1024t = _ctx_1024t * jax.lax.rsqrt(jnp.mean(jnp.square(_ctx_1024t)) + 1e-12) * 0.953939
        ctx_1024 = 2.81802e-05 + 1.00001 * (_ctx_1024t + 0.3 * jax.random.normal(jax.random.fold_in(_rk, 611), (8, 128, 128), jnp.float32))
        _validS = jnp.arange(128)[None, :] < _lenS[:, None]
        _validS2 = jnp.arange(128)[None, :] < _lenS2[:, None]
        _causal = jnp.tril(jnp.ones((128, 128), dtype=bool))
        mask_BxS2_bk1 = jnp.broadcast_to(_validS2[:, :], (8, 128))
        mask_BxS2_bk0 = jnp.logical_not(jnp.broadcast_to(_validS2[:, :], (8, 128)))
        _g = jax.random.normal(jax.random.fold_in(_rk, 9001), (2, 1), jnp.float32)
        _g = jnp.sign(_g) * jnp.maximum(jnp.abs(_g), 1.0) + (_g == 0) * 1.0
        g_xattn = _g[0]
        g_ffn = _g[1]
        return (x, ctx_1024, mask_BxS2_bk1, mask_BxS2_bk0, g_xattn, g_ffn)
    x, ctx_1024, mask_BxS2_bk1, mask_BxS2_bk0, g_xattn, g_ffn = _rec_inputs()

    def _L0_xattn_setup():
        import jax, jax.numpy as jnp
        import numpy as np
        NEG_INF = -2.0 ** 31
        key = jax.random.key(seed)
        kq, kk, kv, kqm, kkm = jax.random.split(key, 5)
        B, Lq, Lk, D = (8, 256, 256, 128)
        return {'query': jax.random.normal(kq, (B, Lq, D), dtype=jnp.float32), 'key': jax.random.normal(kk, (B, Lk, D), dtype=jnp.float32), 'value': jax.random.normal(kv, (B, Lk, D), dtype=jnp.float32), 'query_mask': jax.random.randint(kqm, (B, Lq), 0, 2).astype(bool), 'key_mask': jax.random.randint(kkm, (B, Lk), 0, 2).astype(bool)}
    _L0_xattn_all = _L0_xattn_setup()
    _L0_xattn_in = {k: v for k, v in _L0_xattn_all.items() if k in ()}
    del _L0_xattn_all

    def _L0_ffn_setup():
        import jax, jax.numpy as jnp
        import numpy as np
        import math
        N_EMBD = 128
        HIDDEN = 4 * N_EMBD
        N_EXPERTS = 8
        TOP_K = 2
        B, T = (4, 256)

        def new_gelu(x):
            c = math.sqrt(2.0 / math.pi)
            return 0.5 * x * (1.0 + jnp.tanh(c * (x + 0.044715 * x * x * x)))

        def _moe_forward(x, Wfc_s, bfc_s, Wproj_s, bproj_s, Wr, Wfc, bfc, Wproj, bproj):
            Bb, Tt, C = x.shape
            xf = x.reshape(Bb * Tt, C)
            N = Bb * Tt
            shared = new_gelu(xf @ Wfc_s + bfc_s) @ Wproj_s + bproj_s
            logits = xf @ Wr
            probs = jax.nn.softmax(logits, axis=-1)
            topk_p, topk_i = jax.lax.top_k(probs, TOP_K)
            topk_p = topk_p / jnp.sum(topk_p, axis=-1, keepdims=True)
            gate = jnp.zeros((N, N_EXPERTS), dtype=xf.dtype)
            gate = gate.at[jnp.arange(N)[:, None], topk_i].add(topk_p)
            routed = jnp.zeros_like(xf)
            for e in range(N_EXPERTS):
                h = new_gelu(xf @ Wfc[e] + bfc[e]) @ Wproj[e] + bproj[e]
                routed = routed + h * gate[:, e:e + 1]
            return (shared + routed).reshape(Bb, Tt, C)
        key = jax.random.key(seed)
        ks = jax.random.split(key, 10)
        s = 0.02
        return {'x': jax.random.normal(ks[0], (B, T, N_EMBD), dtype=jnp.float32), 'Wfc_s': jax.random.normal(ks[1], (N_EMBD, HIDDEN), dtype=jnp.float32) * s, 'bfc_s': jnp.zeros((HIDDEN,), dtype=jnp.float32), 'Wproj_s': jax.random.normal(ks[2], (HIDDEN, N_EMBD), dtype=jnp.float32) * s, 'bproj_s': jnp.zeros((N_EMBD,), dtype=jnp.float32), 'Wr': jax.random.normal(ks[3], (N_EMBD, N_EXPERTS), dtype=jnp.float32) * s, 'Wfc': jax.random.normal(ks[4], (N_EXPERTS, N_EMBD, HIDDEN), dtype=jnp.float32) * s, 'bfc': jnp.zeros((N_EXPERTS, HIDDEN), dtype=jnp.float32), 'Wproj': jax.random.normal(ks[5], (N_EXPERTS, HIDDEN, N_EMBD), dtype=jnp.float32) * s, 'bproj': jnp.zeros((N_EXPERTS, N_EMBD), dtype=jnp.float32)}
    _L0_ffn_all = _L0_ffn_setup()
    _L0_ffn_in = {k: v for k, v in _L0_ffn_all.items() if k in ('Wfc_s', 'bfc_s', 'Wproj_s', 'bproj_s', 'Wr', 'Wfc', 'bfc', 'Wproj', 'bproj')}
    del _L0_ffn_all
    return {'x': x, 'ctx_1024': ctx_1024, 'mask_BxS2_bk1': mask_BxS2_bk1, 'mask_BxS2_bk0': mask_BxS2_bk0, 'g_xattn': g_xattn, 'g_ffn': g_ffn, 'L0_ffn_Wfc_s': _L0_ffn_in['Wfc_s'], 'L0_ffn_bfc_s': _L0_ffn_in['bfc_s'], 'L0_ffn_Wproj_s': _L0_ffn_in['Wproj_s'], 'L0_ffn_bproj_s': _L0_ffn_in['bproj_s'], 'L0_ffn_Wr': _L0_ffn_in['Wr'], 'L0_ffn_Wfc': _L0_ffn_in['Wfc'], 'L0_ffn_bfc': _L0_ffn_in['bfc'], 'L0_ffn_Wproj': _L0_ffn_in['Wproj'], 'L0_ffn_bproj': _L0_ffn_in['bproj']}

def reference(x, ctx_1024, mask_BxS2_bk1, mask_BxS2_bk0, g_xattn, g_ffn, L0_ffn_Wfc_s, L0_ffn_bfc_s, L0_ffn_Wproj_s, L0_ffn_bproj_s, L0_ffn_Wr, L0_ffn_Wfc, L0_ffn_bfc, L0_ffn_Wproj, L0_ffn_bproj):
    import jax
    import jax.numpy as jnp

    def _L0_xattn_ref(query, key, value, query_mask, key_mask):
        import jax, jax.numpy as jnp
        import numpy as np
        NEG_INF = -2.0 ** 31
        D = value.shape[2]
        scale = jnp.sqrt(jnp.float32(D))
        scores = jnp.einsum('bqd,bkd->bqk', query, key) / scale
        attn_mask = query_mask[:, :, None] & key_mask[:, None, :]
        scores = jnp.where(attn_mask, scores, NEG_INF)
        probs = jax.nn.softmax(scores, axis=-1)
        probs = jnp.where(attn_mask, probs, 0.0)
        return jnp.einsum('bqk,bkd->bqd', probs, value)

    def _L0_ffn_ref(x, Wfc_s, bfc_s, Wproj_s, bproj_s, Wr, Wfc, bfc, Wproj, bproj):
        import jax, jax.numpy as jnp
        import numpy as np
        import math
        N_EMBD = 128
        HIDDEN = 4 * N_EMBD
        N_EXPERTS = 8
        TOP_K = 2
        B, T = (4, 256)

        def new_gelu(x):
            c = math.sqrt(2.0 / math.pi)
            return 0.5 * x * (1.0 + jnp.tanh(c * (x + 0.044715 * x * x * x)))

        def _moe_forward(x, Wfc_s, bfc_s, Wproj_s, bproj_s, Wr, Wfc, bfc, Wproj, bproj):
            Bb, Tt, C = x.shape
            xf = x.reshape(Bb * Tt, C)
            N = Bb * Tt
            shared = new_gelu(xf @ Wfc_s + bfc_s) @ Wproj_s + bproj_s
            logits = xf @ Wr
            probs = jax.nn.softmax(logits, axis=-1)
            topk_p, topk_i = jax.lax.top_k(probs, TOP_K)
            topk_p = topk_p / jnp.sum(topk_p, axis=-1, keepdims=True)
            gate = jnp.zeros((N, N_EXPERTS), dtype=xf.dtype)
            gate = gate.at[jnp.arange(N)[:, None], topk_i].add(topk_p)
            routed = jnp.zeros_like(xf)
            for e in range(N_EXPERTS):
                h = new_gelu(xf @ Wfc[e] + bfc[e]) @ Wproj[e] + bproj[e]
                routed = routed + h * gate[:, e:e + 1]
            return (shared + routed).reshape(Bb, Tt, C)
        return _moe_forward(x, Wfc_s, bfc_s, Wproj_s, bproj_s, Wr, Wfc, bfc, Wproj, bproj)
    x = x + jnp.tanh(g_xattn[0]) * _L0_xattn_ref(_layernorm(x, axis=-1), ctx_1024, ctx_1024, mask_BxS2_bk1, mask_BxS2_bk0)
    x = x + jnp.tanh(g_ffn[0]) * _L0_ffn_ref(_layernorm(x, axis=-1), L0_ffn_Wfc_s, L0_ffn_bfc_s, L0_ffn_Wproj_s, L0_ffn_bproj_s, L0_ffn_Wr, L0_ffn_Wfc, L0_ffn_bfc, L0_ffn_Wproj, L0_ffn_bproj)
    return x

_drawn_inputs = setup_inputs


def setup_inputs(seed=0):
    import zlib

    import numpy as np

    out = dict(_drawn_inputs(seed))
    spreads = {'L0_ffn_bfc_s': (0.0, 0.362),
     'L0_ffn_bproj_s': (0.0, 0.1),
     'L0_ffn_bfc': (0.0, 0.576),
     'L0_ffn_bproj': (0.0, 0.1)}
    factors = {}
    for name, (base, spread) in spreads.items():
        noise = np.random.default_rng([zlib.crc32(name.encode()), seed]).standard_normal(out[name].shape)
        drawn = base * np.exp(spread * noise) if base else spread * noise
        out[name] = jnp.asarray(drawn.astype(out[name].dtype))
    for name, factor in factors.items():
        out[name] = (out[name] * factor).astype(out[name].dtype)
    return out
```

```python
from contextlib import ExitStack

import concourse.bass as bass
from concourse import mybir

F32 = mybir.dt.float32
F32R = mybir.dt.float32r
BF16 = mybir.dt.bfloat16
U8 = mybir.dt.uint8
U32 = mybir.dt.uint32
ALU = mybir.AluOpType
ACT = mybir.ActivationFunctionType
AX_X = mybir.AxisListType.X

LN_EPS = 1e-5
MASK_NEG = -(2.0 ** 35)
RING = 8
LAG = 3


def flamingo_gated_moe(nc, x, ctx_in, q_mask, k_mask, g_xattn, g_ffn,
                       Wfc_s, bfc_s, Wproj_s, bproj_s, Wr, Wfc, bfc, Wproj, bproj, out):
    B, S, D = x.shape
    E, _, HID = Wfc.shape
    P = 128
    HALVES = 2
    BH = B // HALVES
    N = BH * S
    C = HID // P
    PAIR = 2 * HALVES * C
    FIRST = HALVES * C
    SCALE = float(D) ** -0.5
    assert S == P and D == P and N == 512 and E % 2 == 0 and C == 4

    gates_dram = nc.dram_tensor("gates_scratch", (E, B * S), F32, kind="Internal").ap()

    with ExitStack() as ctx:
        def sb(name, shape, dt=F32):
            return ctx.enter_context(nc.sbuf_tensor(name, shape, dt))

        def sem(name):
            return ctx.enter_context(nc.semaphore(name))

        x_sb = sb("x_sb", [P, B, D])
        ctx_sb = sb("ctx_sb", [P, B, D])
        xn = sb("xn", [P, B, D])
        ctxT = sb("ctxT", [P, B, S])
        xnT = sb("xnT", [P, B, S])
        v_masked = sb("v_masked", [P, B, D])
        probs = sb("probs", [P, B, S])
        probsT = sb("probsT", [P, B, S])
        x2 = sb("x2", [P, B, D])
        x2n = sb("x2n", [P, B, D])
        tok_hi = sb("tok_hi", [P, HALVES, N], F32R)
        tok_lo = sb("tok_lo", [P, HALVES, N], F32R)
        stats = sb("stats", [P, B, 6])
        moments1 = sb("moments1", [P, B, 2])
        moments2 = sb("moments2", [P, B, 2])
        var_eps = sb("var_eps", [P, 2, B])
        rstd = sb("rstd", [P, 2, B])
        minus_half = sb("minus_half", [P, BH])
        smax = sb("smax", [P, B])
        neg_max = sb("neg_max", [P, B])
        denom = sb("denom", [P, B])
        inv_denom = sb("inv_denom", [P, B])
        row_scale = sb("row_scale", [P, B])
        ident = sb("ident", [P, P])
        ones_row = sb("ones_row", [1, P], BF16)
        mask_words = sb("mask_words", [2 * B, S // 4], U32)
        mask_rows_f = sb("mask_rows_f", [2 * B, S])
        maskT = sb("maskT", [P, 2 * B])
        k_words = sb("k_words", [1, B * S // 4], U32)
        neg_row = sb("neg_row", [1, B * S], BF16)
        q_scale = sb("q_scale", [P, B])
        g_raw = sb("g_raw", [P, 2])
        g_tanh = sb("g_tanh", [P, 2])
        BIAS_ROWS = (E + 1) * (C + 1)
        FC_S, PJ_E, PJ_S = E * C, (E + 1) * C, (E + 1) * C + E
        bias_rows = sb("bias_rows", [BIAS_ROWS, P])
        biasT = sb("biasT", [P, BIAS_ROWS])
        wr_raw = sb("wr_raw", [P, E])
        wr_hi = sb("wr_hi", [P, E], F32R)
        wr_lo = sb("wr_lo", [P, E], F32R)
        top = sb("top", [P, B, 8])
        top_idx = sb("top_idx", [P, B, 8], U32)
        top_idx_f = sb("top_idx_f", [P, B, 2])
        logits_sb = sb("logits_sb", [P, B, E])
        top_diff = sb("top_diff", [P, B])
        top_tanh = sb("top_tanh", [P, B])
        gate_top = sb("gate_top", [P, 2, B])
        expert_id = sb("expert_id", [P, BH, E])
        pick1 = sb("pick1", [P, B, E])
        pick2 = sb("pick2", [P, B, E])
        gates = sb("gates", [P, B, E])
        gatesT = sb("gatesT", [E, HALVES, N])
        fc_raw = [sb(f"fc_raw{s}", [P, HID]) for s in range(2)]
        pj_raw = [sb(f"pj_raw{s}", [P, HID]) for s in range(2)]
        fc_hi = [sb(f"fc_hi{s}", [P, HID], F32R) for s in range(2)]
        fc_lo = [sb(f"fc_lo{s}", [P, HID], F32R) for s in range(2)]
        pj_hi = [sb(f"pj_hi{s}", [P, HID], F32R) for s in range(2)]
        pj_lo = [sb(f"pj_lo{s}", [P, HID], F32R) for s in range(2)]
        fc_bias = [sb(f"fc_bias{s}", [P, C]) for s in range(2)]
        pj_bias = [sb(f"pj_bias{s}", [P, 1]) for s in range(2)]
        gate_bc = [sb(f"gate_bc{s}", [P, HALVES * N]) for s in range(2)]
        hid = sb("hid", [P, RING, N])
        hid_hi = sb("hid_hi", [P, RING, N], F32R)
        hid_lo = sb("hid_lo", [P, RING, N], F32R)
        gated = sb("gated", [P, HALVES, N])
        acc = sb("acc", [P, HALVES, N])
        y = sb("y", [P, B, D])

        ps_h = [ctx.enter_context(nc.psum_tensor(f"ps_h{i}", [P, N], F32)) for i in range(4)]
        ps_o = [ctx.enter_context(nc.psum_tensor(f"ps_o{i}", [P, N], F32)) for i in range(HALVES)]
        ps_m = [ctx.enter_context(nc.psum_tensor(f"ps_m{i}", [P, N], F32)) for i in range(2)]
        ps_ctxT, ps_xnT = [ps_h[0], ps_h[1]], [ps_h[2], ps_h[3]]
        ps_scores = ps_o
        ps_probsT, ps_att = [ps_h[0], ps_m[0]], [ps_h[1], ps_m[1]]
        ps_tokT = [ps_h[2], ps_m[0]]
        ps_masks = ps_m[0][:, 0:2 * B]
        ps_bias = ps_m[1][:, 0:BIAS_ROWS]
        ps_logits = [ps_m[1][:, 0:BH * E], ps_m[0][:, 0:BH * E]]
        ps_gatesT = [ps_m[1], ps_m[0]]

        x_in = [sem(f"x_in{h}") for h in range(HALVES)]
        ctx_ld = [sem(f"ctx_ld{h}") for h in range(HALVES)]
        masks_in, krow_in, g_in, bias_in, wr_in = sem("masks_in"), sem("krow_in"), sem("g_in"), sem("bias_in"), sem("wr_in")
        fc_in = [sem(f"fc_in{s}") for s in range(2)]
        pj_in = [sem(f"pj_in{s}") for s in range(2)]
        gate_in = [sem(f"gate_in{s}") for s in range(2)]
        gates_stored = sem("gates_stored")
        out_stored = sem("out_stored")
        ident_zero, ident_ready, consts_ready = sem("ident_zero"), sem("ident_ready"), sem("consts_ready")
        ones_ready, mask_f_ready, neg_ready = sem("ones_ready"), sem("mask_f_ready"), sem("neg_ready")
        masks_ps, maskT_ready, bias_ps, biasT_ready = sem("masks_ps"), sem("maskT_ready"), sem("bias_ps"), sem("biasT_ready")
        g_ready, wr_ready = sem("g_ready"), sem("wr_ready")
        var1_ready, rstd1_ready, var2_ready, rstd2_ready = sem("var1_ready"), sem("rstd1_ready"), sem("var2_ready"), sem("rstd2_ready")
        xn_ready, x2n_ready = sem("xn_ready"), sem("x2n_ready")
        ctxT_ps, ctxT_ready, xnT_ps, xnT_ready = sem("ctxT_ps"), sem("ctxT_ready"), sem("xnT_ps"), sem("xnT_ready")
        scores_ps, neg_max_ready, probs_ready = sem("scores_ps"), sem("neg_max_ready"), sem("probs_ready")
        v_ready, probsT_ps, probsT_ready, att_ps, x2_ready = sem("v_ready"), sem("probsT_ps"), sem("probsT_ready"), sem("att_ps"), sem("x2_ready")
        tokT_ps, tok_hi_ready, tok_ready = sem("tokT_ps"), sem("tok_hi_ready"), sem("tok_ready")
        logits_ps, diff_ready, tanh_ready, gates_ready = sem("logits_ps"), sem("diff_ready"), sem("tanh_ready"), sem("gates_ready")
        gatesT_ps, gatesT_ready = sem("gatesT_ps"), sem("gatesT_ready")
        dve_step = sem("dve_step")
        hi_split, fc_ready, pj_ready = sem("hi_split"), sem("fc_ready"), sem("pj_ready")
        fc_done, gelu_done, hi_cast, lo_done, pj_done = sem("fc_done"), sem("gelu_done"), sem("hi_cast"), sem("lo_done"), sem("pj_done")
        gated_done, acc_added, acc_last = sem("gated_done"), sem("acc_added"), sem("acc_last")
        y_ps, y_ready = sem("y_ps"), sem("y_ready")

        def half(t, h):
            return t[:, h * BH:(h + 1) * BH, :]

        def flat(t, h):
            return half(t, h).rearrange("p b d -> p (b d)")

        def at_least(eng, s, value):
            if not isinstance(value, int) or value > 0:
                eng.wait_ge(s, value)

        block = ctx.enter_context(nc.Block())

        @block.sync
        def _(sp):
            def weights(slot, fc, pj):
                sp.dma_start(fc_raw[slot][:, :], fc).then_inc(fc_in[slot], 16)
                sp.dma_start(pj_raw[slot][:, :].rearrange("p (c d) -> p c d", c=C),
                             pj.rearrange("(c p) d -> p c d", p=P)).then_inc(pj_in[slot], 16)

            def expert(slot, e):
                weights(slot, Wfc[bass.ds(e, 1), :, :].rearrange("e p n -> (e p) n"),
                        Wproj[bass.ds(e, 1), :, :].rearrange("e h d -> (e h) d"))

            def gate(slot, e):
                row = gates_dram[bass.ds(e, 1), :]
                sp.dma_start(gate_bc[slot][:, :], row.to_broadcast([P, B * S])).then_inc(gate_in[slot], 16)

            for h in range(HALVES):
                sp.dma_start(half(x_sb, h), x[h * BH:(h + 1) * BH, :, :].rearrange("b p d -> p b d")).then_inc(x_in[h], 16)
            sp.dma_start(bias_rows[0:FC_S, :], bfc.rearrange("e (c p) -> (e c) p", p=P)).then_inc(bias_in, 16)
            sp.dma_start(bias_rows[FC_S:PJ_E, :], bfc_s.rearrange("(c p) -> c p", p=P)).then_inc(bias_in, 16)
            sp.dma_start(bias_rows[PJ_E:PJ_S, :], bproj).then_inc(bias_in, 16)
            sp.dma_start(bias_rows[PJ_S:PJ_S + 1, :], bproj_s.rearrange("(a p) -> a p", a=1)).then_inc(bias_in, 16)
            weights(1, Wfc_s, Wproj_s)
            weights(0, Wfc[0, :, :], Wproj[0, :, :])
            sp.wait_ge(fc_ready, 1)
            sp.wait_ge(pj_ready, 1)
            weights(1, Wfc[1, :, :], Wproj[1, :, :])
            for h in range(HALVES):
                sp.wait_ge(gatesT_ready, h + 1)
                sp.dma_start(gates_dram[:, h * N:(h + 1) * N], gatesT[:, h, :]).then_inc(gates_stored, 16)
            sp.wait_ge(gates_stored, 16 * HALVES)

            def expert_pair(it, more):
                sp.wait_ge(gated_done, 4 * it + 1)
                gate(0, 2 * it)
                if more:
                    sp.wait_ge(fc_ready, 2 * it + 2)
                    sp.wait_ge(pj_ready, 2 * it + 2)
                    expert(0, 2 * it + 2)
                sp.wait_ge(gated_done, 4 * it + 2)
                gate(1, 2 * it + 1)
                if more:
                    sp.wait_ge(fc_ready, 2 * it + 3)
                    sp.wait_ge(pj_ready, 2 * it + 3)
                    expert(1, 2 * it + 3)

            with sp.Fori(0, E // 2 - 1) as it:
                expert_pair(it, True)
            expert_pair(E // 2 - 1, False)
            for h in range(HALVES):
                sp.wait_ge(y_ready, h + 1)
                sp.dma_start(out[h * BH:(h + 1) * BH, :, :].rearrange("b p d -> p b d"), half(y, h)).then_inc(out_stored, 16)
            sp.wait_ge(out_stored, 16 * HALVES)

        @block.tensor
        def _(pe):
            def transposes(ps, src, h, ready):
                for b in range(BH):
                    last = nc.tensor.transpose(ps[:, b * P:(b + 1) * P], src[:, h * BH + b, :], ident[:, :])
                last.then_inc(ready, 1)

            pe.wait_ge(ident_ready, 1)
            pe.wait_ge(mask_f_ready, 1)
            nc.tensor.transpose(ps_masks, mask_rows_f[:, :], ident[0:2 * B, 0:2 * B]).then_inc(masks_ps, 1)
            pe.wait_ge(ones_ready, 1)
            pe.wait_ge(neg_ready, 1)
            for h in range(HALVES):
                nc.tensor.matmul(ps_scores[h][:, :], ones_row[:, :], neg_row[:, h * N:(h + 1) * N], start=True, stop=False)
            for h in range(HALVES):
                pe.wait_ge(ctx_ld[h], 16)
                transposes(ps_ctxT[h], ctx_sb, h, ctxT_ps)
            for h in range(HALVES):
                pe.wait_ge(xn_ready, h + 1)
                transposes(ps_xnT[h], xn, h, xnT_ps)
                if h == 0:
                    pe.wait_ge(bias_in, 64)
                    nc.tensor.transpose(ps_bias, bias_rows[:, :], ident[0:BIAS_ROWS, 0:BIAS_ROWS]).then_inc(bias_ps, 1)
                pe.wait_ge(ctxT_ready, h + 1)
                pe.wait_ge(xnT_ready, h + 1)
                for b in range(BH):
                    last = nc.tensor.matmul(ps_scores[h][:, b * P:(b + 1) * P], xnT[:, h * BH + b, :],
                                            ctxT[:, h * BH + b, :], start=False, stop=(b == BH - 1))
                last.then_inc(scores_ps, 1)
            for h in range(HALVES):
                pe.wait_ge(probs_ready, h + 1)
                if h == 1:
                    pe.wait_ge(maskT_ready, 1)
                transposes(ps_probsT[h], probs, h, probsT_ps)
                pe.wait_ge(probsT_ready, h + 1)
                pe.wait_ge(v_ready, h + 1)
                if h == 1:
                    pe.wait_ge(biasT_ready, 1)
                for b in range(BH):
                    last = nc.tensor.matmul(ps_att[h][:, b * P:(b + 1) * P], probsT[:, h * BH + b, :],
                                            v_masked[:, h * BH + b, :], start=True, stop=True)
                last.then_inc(att_ps, 1)

            def three_passes(ps, w_hi, w_lo, m_hi, m_lo, start, stop):
                nc.tensor.matmul(ps, w_hi, m_hi, start=start, stop=False)
                nc.tensor.matmul(ps, w_hi, m_lo, start=False, stop=False)
                return nc.tensor.matmul(ps, w_lo, m_hi, start=False, stop=stop)

            def first_product(slot, h, c, g):
                at_least(pe, gelu_done, g - 3)
                cols = slice(c * P, (c + 1) * P)
                three_passes(ps_h[c][:, :], fc_hi[slot][:, cols], fc_lo[slot][:, cols],
                             tok_hi[:, h, :], tok_lo[:, h, :], True, True).then_inc(fc_done, 1)

            def second_product(slot, h, c, g, r):
                pe.wait_ge(lo_done, g + 1)
                cols = slice(c * P, (c + 1) * P)
                three_passes(ps_o[h][:, :], pj_hi[slot][:, cols], pj_lo[slot][:, cols],
                             hid_hi[:, r, :], hid_lo[:, r, :], c == 0, c == C - 1).then_inc(pj_done, 1)

            def logits(h):
                for b in range(BH):
                    o = ps_logits[h][:, b * E:(b + 1) * E]
                    cols = slice(b * P, (b + 1) * P)
                    last = three_passes(o, tok_hi[:, h, cols], tok_lo[:, h, cols], wr_hi[:, :], wr_lo[:, :], True, True)
                last.then_inc(logits_ps, 1)

            def gates_transposed(h):
                pe.wait_ge(gates_ready, h + 1)
                for b in range(BH):
                    last = nc.tensor.transpose(ps_gatesT[h][0:E, b * P:(b + 1) * P], gates[:, h * BH + b, :], ident[:, :])
                last.then_inc(gatesT_ps, 1)

            pe.wait_ge(x2n_ready, 1)
            transposes(ps_tokT[0], x2n, 0, tokT_ps)
            pe.wait_ge(fc_ready, 1)
            for g in range(FIRST):
                h, c = g // C, g % C
                if c == 0:
                    pe.wait_ge(tok_ready, h + 1)
                if g == 0:
                    pe.wait_ge(x2_ready, 1)
                first_product(1, h, c, g)
                if g == 1:
                    pe.wait_ge(x2n_ready, 2)
                    transposes(ps_tokT[1], x2n, 1, tokT_ps)
                if g == LAG:
                    pe.wait_ge(pj_ready, 1)
                if g >= LAG:
                    second_product(1, (g - LAG) // C, (g - LAG) % C, g - LAG, (g - LAG) % RING)
                if g == 3:
                    pe.wait_ge(wr_ready, 1)
                    pe.wait_ge(x2_ready, 2)
                    logits(0)
                if g == 4:
                    logits(1)
                if g >= FIRST - HALVES:
                    gates_transposed(g - FIRST + HALVES)

            with pe.Fori(0, E // 2) as it:
                for k in range(PAIR):
                    g = PAIR * it + (FIRST + k)
                    slot, h, c = k // FIRST, k // C % HALVES, k % C
                    if k % FIRST == 0:
                        pe.wait_ge(fc_ready, 2 * it + (2 + slot))
                    first_product(slot, h, c, g)
                    j = k - LAG
                    if j % FIRST == 0:
                        pe.wait_ge(pj_ready, 2 * it + (2 + slot))
                    if j % C == 0:
                        pe.wait_ge(gated_done, 4 * it + (1 + j // C))
                    second_product(j // FIRST % 2, j // C % HALVES, j % C, g - LAG, j % RING)
            total = FIRST + PAIR * (E // 2)
            for g in range(total - LAG, total):
                second_product(1, 1, g % C, g, g % RING)
            for h in range(HALVES):
                if h == 0:
                    pe.wait_ge(acc_added, 2 * E + 2)
                    pe.wait_ge(gatesT_ready, HALVES)
                else:
                    pe.wait_ge(acc_last, 1)
                for b in range(BH):
                    last = nc.tensor.transpose(ps_m[h][:, b * P:(b + 1) * P], acc[:, h, b * P:(b + 1) * P], ident[:, :])
                last.then_inc(y_ps, 1)

        @block.scalar
        def _(act):
            act.dma_start(mask_words[0:B, :], q_mask).then_inc(masks_in, 16)
            act.dma_start(mask_words[B:2 * B, :], k_mask).then_inc(masks_in, 16)
            act.dma_start(k_words[:, :], k_mask.rearrange("b (a s) -> a (b s)", a=1)).then_inc(krow_in, 16)
            for h in range(HALVES):
                act.dma_start(half(ctx_sb, h), ctx_in[h * BH:(h + 1) * BH, :, :].rearrange("b p d -> p b d")).then_inc(ctx_ld[h], 16)
            act.dma_start(g_raw[:, 0:1], g_xattn.rearrange("(a b) -> a b", a=1).to_broadcast([P, 1])).then_inc(g_in, 16)
            act.dma_start(g_raw[:, 1:2], g_ffn.rearrange("(a b) -> a b", a=1).to_broadcast([P, 1])).then_inc(g_in, 16)
            act.dma_start(wr_raw[:, :], Wr).then_inc(wr_in, 16)

            def evacuate(dst, ps, full, done):
                act.wait_ge(full[0], full[1])
                nc.scalar.activation(dst, ps, ACT.Copy).then_inc(done, 1)

            evacuate(maskT[:, :], ps_masks, (masks_ps, 1), maskT_ready)
            act.wait_ge(g_in, 32)
            nc.scalar.activation(g_tanh[:, :], g_raw[:, :], ACT.Tanh).then_inc(g_ready, 1)
            for h in range(HALVES):
                evacuate(flat(ctxT, h), ps_ctxT[h][:, :], (ctxT_ps, h + 1), ctxT_ready)
            act.wait_ge(maskT_ready, 1)
            for h in range(HALVES):
                evacuate(flat(xnT, h), ps_xnT[h][:, :], (xnT_ps, h + 1), xnT_ready)
                for b in range(h * BH, (h + 1) * BH):
                    last = nc.scalar.activation(v_masked[:, b, :], ctx_sb[:, b, :], ACT.Copy, scale=maskT[:, B + b:B + b + 1])
                last.then_inc(v_ready, 1)
            evacuate(biasT[:, :], ps_bias, (bias_ps, 1), biasT_ready)
            for h in range(HALVES):
                act.wait_ge(neg_max_ready, h + 1)
                for b in range(h * BH, (h + 1) * BH):
                    last = nc.scalar.activation(probs[:, b, :], ps_scores[h][:, (b - h * BH) * P:(b - h * BH + 1) * P], ACT.Exp,
                                                bias=neg_max[:, b:b + 1], scale=SCALE, accum_out=denom[:, b:b + 1])
                last.then_inc(probs_ready, 1)
            for h in range(HALVES):
                evacuate(flat(probsT, h), ps_probsT[h][:, :], (probsT_ps, h + 1), probsT_ready)
            evacuate(tok_hi[:, 0, :], ps_tokT[0][:, :], (tokT_ps, 1), tok_hi_ready)

            def gelu(slot, h, c, g, r):
                act.wait_ge(fc_done, g + 1)
                at_least(act, pj_done, g - RING + 1)
                if c % 2 == 0:
                    nc.scalar.activation(hid_hi[:, r, :], ps_h[c][:, :], ACT.Gelu_apprx_tanh, bias=fc_bias[slot][:, c:c + 1])
                nc.scalar.activation(hid[:, r, :], ps_h[c][:, :], ACT.Gelu_apprx_tanh,
                                     bias=fc_bias[slot][:, c:c + 1]).then_inc(gelu_done, 1)

            for g in range(FIRST):
                gelu(1, g // C, g % C, g, g % RING)
                if g == 1:
                    evacuate(tok_hi[:, 1, :], ps_tokT[1][:, :], (tokT_ps, 2), tok_hi_ready)
                if g >= FIRST - 3 and g < FIRST - 1:
                    h = g - FIRST + 3
                    act.wait_ge(diff_ready, h + 1)
                    nc.scalar.activation(top_tanh[:, h * BH:(h + 1) * BH], top_diff[:, h * BH:(h + 1) * BH], ACT.Tanh,
                                         scale=0.5).then_inc(tanh_ready, 1)
            for h in range(HALVES):
                evacuate(gatesT[:, h, :], ps_gatesT[h][0:E, :], (gatesT_ps, h + 1), gatesT_ready)
            with act.Fori(0, E // 2) as it:
                for k in range(PAIR):
                    gelu(k // FIRST, k // C % HALVES, k % C, PAIR * it + (FIRST + k), k % RING)

        @block.vector
        def _(dve):
            steps = [0]

            def chain(ins):
                steps[0] += 1
                ins.then_inc(dve_step, 1)
                dve.wait_ge(dve_step, steps[0])

            def variance(src, h, moments, var, ready):
                for b in range(h * BH, (h + 1) * BH):
                    last = nc.vector.bn_stats(stats[:, b, :], src[:, b, :])
                chain(last)
                for b in range(h * BH, (h + 1) * BH):
                    last = nc.vector.bn_aggr(moments[:, b, :], stats[:, b, :])
                chain(last)
                nc.vector.tensor_scalar(var[:, h * BH:(h + 1) * BH], moments[:, h * BH:(h + 1) * BH, 1],
                                        LN_EPS, None, ALU.add).then_inc(ready, 1)

            def normalise(dst, src, h, moments, r, ready):
                for b in range(h * BH, (h + 1) * BH):
                    last = nc.vector.tensor_scalar(dst[:, b, :], src[:, b, :], moments[:, b, 0:1], r[:, b:b + 1],
                                                   ALU.subtract, ALU.mult)
                last.then_inc(ready, 1)

            nc.vector.memset(ones_row[:, :], 1.0).then_inc(ones_ready, 1)
            dve.wait_ge(masks_in, 32)
            nc.vector.tensor_copy(mask_rows_f[:, :], mask_words[:, :].bitcast(U8)).then_inc(mask_f_ready, 1)
            dve.wait_ge(krow_in, 16)
            nc.vector.tensor_scalar(neg_row[:, :], k_words[:, :].bitcast(U8), -MASK_NEG, MASK_NEG, ALU.mult, ALU.add).then_inc(neg_ready, 1)
            for h in range(HALVES):
                dve.wait_ge(x_in[h], 16)
                variance(x_sb, h, moments1, var_eps[:, 0, :], var1_ready)
            for h in range(HALVES):
                dve.wait_ge(rstd1_ready, h + 1)
                normalise(xn, x_sb, h, moments1, rstd[:, 0, :], xn_ready)
            dve.wait_ge(g_ready, 1)
            dve.wait_ge(maskT_ready, 1)
            chain(nc.vector.tensor_scalar(q_scale[:, :], maskT[:, 0:B], g_tanh[:, 0:1], None, ALU.mult))
            dve.wait_ge(wr_in, 16)
            chain(nc.vector.tensor_copy(wr_hi[:, :], wr_raw[:, :]))
            nc.vector.tensor_tensor(wr_lo[:, :], wr_raw[:, :], wr_hi[:, :].bitcast(F32), ALU.subtract).then_inc(wr_ready, 1)
            for h in range(HALVES):
                cols = slice(h * BH, (h + 1) * BH)
                dve.wait_ge(scores_ps, h + 1)
                chain(nc.vector.reduce_max(smax[:, cols], ps_scores[h][:, :].rearrange("p (b k) -> p b k", b=BH), AX_X))
                nc.vector.tensor_scalar(neg_max[:, cols], smax[:, cols], -SCALE, None, ALU.mult).then_inc(neg_max_ready, 1)

            def residual_attention(h):
                cols = slice(h * BH, (h + 1) * BH)
                dve.wait_ge(probs_ready, h + 1)
                chain(nc.vector.reciprocal(inv_denom[:, cols], denom[:, cols]))
                chain(nc.vector.tensor_tensor(row_scale[:, cols], inv_denom[:, cols], q_scale[:, cols], ALU.mult))
                dve.wait_ge(att_ps, h + 1)
                for b in range(h * BH, (h + 1) * BH):
                    last = nc.vector.scalar_tensor_tensor(x2[:, b, :], ps_att[h][:, (b - h * BH) * P:(b - h * BH + 1) * P],
                                                          row_scale[:, b:b + 1], x_sb[:, b, :], ALU.mult, ALU.add)
                last.then_inc(x2_ready, 1)
                dve.wait_ge(x2_ready, h + 1)
                variance(x2, h, moments2, var_eps[:, 1, :], var2_ready)

            def split_tokens(h):
                dve.wait_ge(tok_hi_ready, h + 1)
                nc.vector.tensor_tensor(tok_lo[:, h, :], ps_tokT[h][:, :], tok_hi[:, h, :].bitcast(F32),
                                        ALU.subtract).then_inc(tok_ready, 1)

            residual_attention(0)
            dve.wait_ge(rstd2_ready, 1)
            normalise(x2n, x2, 0, moments2, rstd[:, 1, :], x2n_ready)
            residual_attention(1)
            split_tokens(0)
            dve.wait_ge(rstd2_ready, 2)
            normalise(x2n, x2, 1, moments2, rstd[:, 1, :], x2n_ready)

            def lower_part(c, g, r):
                dve.wait_ge(gelu_done, g + 1)
                at_least(dve, pj_done, g - RING + 1)
                if c % 2:
                    nc.vector.tensor_copy(hid_hi[:, r, :], hid[:, r, :]).then_inc(hi_cast, 1)
                    dve.wait_ge(hi_cast, (g - c) // 2 + c // 2 + 1 if isinstance(g, int) else hi_count(g))
                nc.vector.tensor_tensor(hid_lo[:, r, :], hid[:, r, :], hid_hi[:, r, :].bitcast(F32),
                                        ALU.subtract).then_inc(lo_done, 1)

            def gate_unit(slot, h, u, loads):
                dve.wait_ge(pj_done, 4 * u + 4)
                if loads is not None:
                    dve.wait_ge(gate_in[slot], loads)
                at_least(dve, acc_added, u)
                nc.vector.scalar_tensor_tensor(gated[:, h, :], ps_o[h][:, :], pj_bias[slot][:, 0:1],
                                               gate_bc[slot][:, h * N:(h + 1) * N], ALU.add, ALU.mult).then_inc(gated_done, 1)

            def top_two(h):
                cols = slice(h * BH, (h + 1) * BH)
                dve.wait_ge(logits_ps, h + 1)
                chain(nc.vector.tensor_copy(flat(logits_sb, h), ps_logits[h]))
                for b in range(h * BH, (h + 1) * BH):
                    last = nc.vector.max(top[:, b, :], logits_sb[:, b, :])
                chain(last)
                nc.vector.tensor_tensor(top_diff[:, cols], top[:, cols, 0], top[:, cols, 1], ALU.subtract).then_inc(diff_ready, 1)
                for b in range(h * BH, (h + 1) * BH):
                    last = nc.vector.max_index(top_idx[:, b, :], top[:, b, :], logits_sb[:, b, :])
                chain(last)
                chain(nc.vector.tensor_copy(top_idx_f[:, cols, :], top_idx[:, cols, 0:2]))
                for pick, k in ((pick1, 0), (pick2, 1)):
                    last = nc.vector.tensor_tensor(half(pick, h), expert_id[:, :, :],
                                                   top_idx_f[:, cols, k:k + 1].to_broadcast([P, BH, E]), ALU.is_equal)
                chain(last)

            def route(h):
                cols = slice(h * BH, (h + 1) * BH)
                dve.wait_ge(tanh_ready, h + 1)
                nc.vector.tensor_scalar(gate_top[:, 0, cols], top_tanh[:, cols], 0.5, 0.5, ALU.mult, ALU.add)
                chain(nc.vector.tensor_scalar(gate_top[:, 1, cols], top_tanh[:, cols], -0.5, 0.5, ALU.mult, ALU.add))
                for pick, k in ((pick1, 0), (pick2, 1)):
                    last = nc.vector.tensor_tensor(half(pick, h), half(pick, h),
                                                   gate_top[:, k, cols].rearrange("p (b o) -> p b o", o=1).to_broadcast([P, BH, E]),
                                                   ALU.mult)
                chain(last)
                nc.vector.tensor_tensor(half(gates, h), half(pick1, h), half(pick2, h), ALU.add).then_inc(gates_ready, 1)

            dve.wait_ge(consts_ready, 1)
            for g in range(FIRST):
                lower_part(g % C, g, g % RING)
                if g == 1:
                    split_tokens(1)
                if g == 3:
                    top_two(0)
                if g == 4:
                    top_two(1)
                if g == 5:
                    route(0)
                if g == 6:
                    route(1)
                    gate_unit(1, 0, 0, None)

            with dve.Fori(0, E // 2) as it:
                for k in range(PAIR):
                    g = PAIR * it + (FIRST + k)
                    def hi_count(_g, k=k):
                        return PAIR // 2 * it + (FIRST // 2 + k // 2 + 1)
                    lower_part(k % C, g, k % RING)
                    if k % C == 2:
                        j = k - LAG - (C - 1)
                        slot, h = j // FIRST % 2, j // C % HALVES
                        u = 4 * it + (FIRST // C + j // C)
                        gate_unit(slot, h, u, 16 * it + (16 if slot == 0 else 16 if j >= 0 else 0) if j >= 0 else None)
            last_unit = 2 * E + 1
            gate_unit(1, 1, last_unit, 16 * (E // 2))
            dve.wait_ge(gated_done, last_unit + 1)
            dve.wait_ge(acc_added, last_unit)
            nc.vector.tensor_tensor(acc[:, 1, :], acc[:, 1, :], gated[:, 1, :], ALU.add).then_inc(acc_last, 1)
            for h in range(HALVES):
                dve.wait_ge(y_ps, h + 1)
                nc.vector.scalar_tensor_tensor(flat(y, h), ps_m[h][:, :], g_tanh[:, 1:2], flat(x2, h),
                                               ALU.mult, ALU.add).then_inc(y_ready, 1)

        @block.gpsimd
        def _(pool):
            nc.gpsimd.memset(ident[:, :], 0.0).then_inc(ident_zero, 1)
            pool.wait_ge(ident_zero, 1)
            nc.gpsimd.affine_select(out=ident[:, :], in_=ident[:, :], compare_op=ALU.not_equal, fill=1.0,
                                    base=0, pattern=[[-1, P]], channel_multiplier=1).then_inc(ident_ready, 1)
            nc.gpsimd.memset(minus_half[:, :], -0.5).then_inc(ident_zero, 1)
            pool.wait_ge(ident_zero, 2)

            def inverse_std(k, h, var_ready, ready):
                cols = slice(h * BH, (h + 1) * BH)
                pool.wait_ge(var_ready, h + 1)
                nc.gpsimd.tensor_tensor(rstd[:, k, cols], var_eps[:, k, cols], minus_half[:, :], ALU.pow).then_inc(ready, 1)

            inverse_std(0, 0, var1_ready, rstd1_ready)
            inverse_std(0, 1, var1_ready, rstd1_ready)
            nc.gpsimd.memset(gate_bc[1][:, :], 1.0)
            for h in range(HALVES):
                last = nc.gpsimd.memset(acc[:, h, :], 0.0)
            last.then_inc(acc_added, 1)
            for e in range(E):
                last = nc.gpsimd.memset(expert_id[:, :, e:e + 1], float(e))
            last.then_inc(consts_ready, 1)

            splits = [0]

            def split(hi, lo, raw, number):
                nc.gpsimd.tensor_copy(hi[:, :], raw[:, :]).then_inc(hi_split, 1)
                pool.wait_ge(hi_split, number)
                return nc.gpsimd.tensor_tensor(lo[:, :], raw[:, :], hi[:, :].bitcast(F32), ALU.subtract)

            def split_fc(slot, loads, n, bias):
                pool.wait_ge(fc_in[slot], loads)
                nc.gpsimd.tensor_copy(fc_bias[slot][:, :], bias)
                split(fc_hi[slot], fc_lo[slot], fc_raw[slot], 2 * n + 1).then_inc(fc_ready, 1)

            def split_pj(slot, loads, n, bias):
                pool.wait_ge(pj_in[slot], loads)
                nc.gpsimd.tensor_copy(pj_bias[slot][:, :], bias)
                split(pj_hi[slot], pj_lo[slot], pj_raw[slot], 2 * n + 2).then_inc(pj_ready, 1)

            def add_unit(h, u):
                pool.wait_ge(gated_done, u + 1)
                at_least(pool, acc_added, u)
                nc.gpsimd.tensor_tensor(acc[:, h, :], acc[:, h, :], gated[:, h, :], ALU.add).then_inc(acc_added, 1)

            pool.wait_ge(biasT_ready, 1)
            split_fc(1, 16, 0, biasT[:, FC_S:PJ_E])
            inverse_std(1, 0, var2_ready, rstd2_ready)
            inverse_std(1, 1, var2_ready, rstd2_ready)
            split_pj(1, 16, 0, biasT[:, PJ_S:PJ_S + 1])
            split_fc(0, 16, 1, biasT[:, 0:C])
            split_pj(0, 16, 1, biasT[:, PJ_E:PJ_E + 1])
            pool.wait_ge(acc_added, 1)
            add_unit(0, 0)

            def expert_pair(it, more):
                e = 2 * it
                pool.wait_ge(fc_done, PAIR * it + FIRST)
                pool.wait_ge(gelu_done, PAIR * it + FIRST)
                split_fc(1, 16 * it + 32, 2 * it + 2, biasT[:, bass.ds(C * e + C, C)])
                add_unit(1, 4 * it + 1)
                pool.wait_ge(pj_done, PAIR * it + FIRST)
                split_pj(1, 16 * it + 32, 2 * it + 2, biasT[:, bass.ds(e + (PJ_E + 1), 1)])
                add_unit(0, 4 * it + 2)
                if more:
                    pool.wait_ge(fc_done, PAIR * it + 2 * FIRST)
                    pool.wait_ge(gelu_done, PAIR * it + 2 * FIRST)
                    split_fc(0, 16 * it + 32, 2 * it + 3, biasT[:, bass.ds(C * e + 2 * C, C)])
                add_unit(1, 4 * it + 3)
                if more:
                    pool.wait_ge(pj_done, PAIR * it + 2 * FIRST)
                    split_pj(0, 16 * it + 32, 2 * it + 3, biasT[:, bass.ds(e + (PJ_E + 2), 1)])
                add_unit(0, 4 * it + 4)

            with pool.Fori(0, E // 2 - 1) as it:
                expert_pair(it, True)
            expert_pair(E // 2 - 1, False)


_INS = ['x', 'ctx_1024', 'mask_BxS2_bk1', 'mask_BxS2_bk0', 'g_xattn', 'g_ffn', 'L0_ffn_Wfc_s', 'L0_ffn_bfc_s',
        'L0_ffn_Wproj_s', 'L0_ffn_bproj_s', 'L0_ffn_Wr', 'L0_ffn_Wfc', 'L0_ffn_bfc', 'L0_ffn_Wproj', 'L0_ffn_bproj']


def kernel(**inputs):
    import numpy as _np
    import concourse.bacc as _bacc
    from concourse import mybir as _mybir
    from concourse.bass_utils import run_bass_kernel_spmd as _run

    nc = _bacc.Bacc("TRN2", target_bir_lowering=False, num_devices=1)
    arrays, args = {}, []
    for name in _INS:
        a = _np.ascontiguousarray(inputs[name])
        if a.dtype == _np.bool_:
            a = a.view(_np.uint32)
        arrays[f"in_{name}"] = a
        args.append(nc.dram_tensor(f"in_{name}", a.shape, _mybir.dt.from_np(a.dtype), kind="ExternalInput").ap())
    out = nc.dram_tensor("out_0", arrays["in_x"].shape, _mybir.dt.float32, kind="ExternalOutput").ap()
    flamingo_gated_moe(nc, *args, out)
    r = _run(nc, [arrays], core_ids=[0])
    return r.results[0]["out_0"]
```

```python
from contextlib import ExitStack

import concourse.bass as bass
from concourse import mybir

F32 = mybir.dt.float32
F32R = mybir.dt.float32r
BF16 = mybir.dt.bfloat16
U8 = mybir.dt.uint8
U32 = mybir.dt.uint32
ALU = mybir.AluOpType
ACT = mybir.ActivationFunctionType
AX_X = mybir.AxisListType.X

LN_EPS = 1e-5
MASK_NEG = -(2.0 ** 100)
RING = 8
WARM_UP = 7
FILL = 8
LAG = 3


def flamingo_gated_moe(nc, x, ctx_in, key_row, per_partition, w_all, out):
    B, S, D = x.shape
    E = w_all.shape[0] - 1
    EXPERTS = E + 1
    P = 128
    HID = w_all.shape[2] // 2
    HALVES = 2
    BH = B // HALVES
    N = BH * S
    C = HID // P
    OF_EXPERT = HALVES * C
    PAIR = 2 * OF_EXPERT
    PEELED = PAIR
    LOOPS = (E - 2) // 2
    CHUNKS = OF_EXPERT * EXPERTS
    UNITS = HALVES * EXPERTS
    FIRST_UNITS = [(0, 0), (1, 0), (0, 1), (1, 1)]
    SCALE = float(D) ** -0.5
    PARTS = [range(0, BH // 2), range(BH // 2, BH), range(BH, B)]
    HALF_PARTS = [2, 3]
    assert S == P and D == P and N == 512 and E % 2 == 0 and C == 4

    gates_dram = nc.dram_tensor("gates_scratch", (E, B * S), F32, kind="Internal").ap()

    with ExitStack() as ctx:
        def sb(name, shape, dt=F32):
            return ctx.enter_context(nc.sbuf_tensor(name, shape, dt))

        def sem(name):
            return ctx.enter_context(nc.semaphore(name))

        x_sb = sb("x_sb", [P, B, D])
        ctx_sb = sb("ctx_sb", [P, B, D])
        xc = sb("xc", [P, B, D])
        ctxT = sb("ctxT", [P, B, S])
        xcT = sb("xcT", [P, B, S])
        v_masked = sb("v_masked", [P, B, D])
        probs = sb("probs", [P, B, S])
        probsT = sb("probsT", [P, B, S])
        x2 = sb("x2", [P, B, D])
        x2n = sb("x2n", [P, B, D])
        tok_hi = sb("tok_hi", [P, HALVES, N], F32R)
        tok_lo = sb("tok_lo", [P, HALVES, N], F32R)
        stats = sb("stats", [P, B, 6])
        moments1 = sb("moments1", [P, B, 2])
        moments2 = sb("moments2", [P, B, 2])
        var_eps = sb("var_eps", [P, 2, B])
        rstd = sb("rstd", [P, 2, B])
        minus_mean = sb("minus_mean", [P, BH])
        minus_half = sb("minus_half", [P, BH])
        exp_scale = sb("exp_scale", [P, B])
        warm = sb("warm", [P, 2])
        smax = sb("smax", [P, B])
        neg_max = sb("neg_max", [P, B])
        denom = sb("denom", [P, B])
        inv_denom = sb("inv_denom", [P, B])
        row_scale = sb("row_scale", [P, B])
        ident = sb("ident", [P, P])
        ones_row = sb("ones_row", [1, P], BF16)
        MASK_W = 2 * B // 4
        BIAS_W = (E + 1) * (C + 1)
        small = sb("small", [P, MASK_W + BIAS_W + E + 2], U32)
        masks_u8 = small[:, 0:MASK_W].bitcast(U8)
        biasT = small[:, MASK_W:MASK_W + BIAS_W].bitcast(F32)
        wr_raw = small[:, MASK_W + BIAS_W:MASK_W + BIAS_W + E].bitcast(F32)
        g_raw = small[:, MASK_W + BIAS_W + E:MASK_W + BIAS_W + E + 2].bitcast(F32)
        mask_f = sb("mask_f", [P, 2 * B])
        key_words = sb("key_words", [1, B * S // 4], U32)
        neg_row = sb("neg_row", [1, B * S], BF16)
        q_scale = sb("q_scale", [P, B])
        g_tanh = sb("g_tanh", [P, 2])
        wr_parts = sb("wr_parts", [P, 2 * E], F32R)
        top = sb("top", [P, B, 8])
        top_idx = sb("top_idx", [P, B, 8], U32)
        top_idx_f = sb("top_idx_f", [P, B, 2])
        logits_sb = sb("logits_sb", [P, B, E])
        top_diff = sb("top_diff", [P, B])
        top_tanh = sb("top_tanh", [P, B])
        gate_top = sb("gate_top", [P, 2, B])
        expert_id = sb("expert_id", [P, E])
        pick1 = sb("pick1", [P, B, E])
        pick2 = sb("pick2", [P, B, E])
        gates = sb("gates", [P, B, E])
        gatesT = sb("gatesT", [E, HALVES, N])
        raw = [sb(f"raw{s}", [P, 2 * HID]) for s in range(2)]
        fc_hi = [sb(f"fc_hi{s}", [P, HID], F32R) for s in range(2)]
        fc_lo = [sb(f"fc_lo{s}", [P, HID], F32R) for s in range(2)]
        pj_hi = [sb(f"pj_hi{s}", [P, HID], F32R) for s in range(2)]
        pj_lo = [sb(f"pj_lo{s}", [P, HID], F32R) for s in range(2)]
        bias = [sb(f"bias{s}", [P, C + 1]) for s in range(2)]
        gate_bc = [sb(f"gate_bc{s}", [P, HALVES * N]) for s in range(2)]
        hid = sb("hid", [P, RING, N])
        hid_hi = sb("hid_hi", [P, RING, N], F32R)
        hid_lo = sb("hid_lo", [P, RING, N], F32R)
        gated = sb("gated", [P, HALVES, N])
        acc = sb("acc", [P, HALVES, N])
        y = sb("y", [P, B, D])

        ps_h = [ctx.enter_context(nc.psum_tensor(f"ps_h{i}", [P, N], F32)) for i in range(4)]
        ps_o = [ctx.enter_context(nc.psum_tensor(f"ps_o{i}", [P, N], F32)) for i in range(HALVES)]
        ps_m = [ctx.enter_context(nc.psum_tensor(f"ps_m{i}", [P, N], F32)) for i in range(2)]
        ps_ctxT = [ps_m[0], ps_m[1]]
        ps_xcT = [ps_h[0], ps_h[1], ps_m[0]]
        ps_scores = [ps_o[0], ps_o[1], ps_m[1]]
        ps_probsT = [ps_h[2], ps_h[3], ps_o[0]]
        ps_att = [ps_h[0], ps_h[1], ps_o[1]]
        ps_tokT = [ps_h[2], ps_h[3], ps_m[0]]
        ps_logits = [ps_m[i][:, 0:BH * 2 * E].rearrange("p (b e) -> p b e", b=BH) for i in (1, 0)]
        ps_gatesT = [ps_m[1], ps_m[0]]

        x_in = [sem(f"x_in{h}") for h in range(HALVES)]
        ctx_ld = [sem(f"ctx_ld{h}") for h in range(HALVES)]
        key_row_in, small_in = sem("key_row_in"), sem("small_in")
        w_in = [sem(f"w_in{s}") for s in range(2)]
        gate_first = sem("gate_first")
        gate_in = [sem(f"gate_in{s}") for s in range(2)]
        gates_stored = sem("gates_stored")
        out_stored = sem("out_stored")
        ident_zero, ident_ready, consts_ready = sem("ident_zero"), sem("ident_ready"), sem("consts_ready")
        ones_ready, mask_f_ready, neg_ready, warm_ready = sem("ones_ready"), sem("mask_f_ready"), sem("neg_ready"), sem("warm_ready")
        g_ready, wr_ready = sem("g_ready"), sem("wr_ready")
        var1_ready, rstd1_ready, var2_ready, rstd2_ready = sem("var1_ready"), sem("rstd1_ready"), sem("var2_ready"), sem("rstd2_ready")
        ctxT_ps, ctxT_ready, v_ready = sem("ctxT_ps"), sem("ctxT_ready"), sem("v_ready")
        logits_ps, top_ready, index_ready, tanh_ready, picks_ready, gates_ready = sem("logits_ps"), sem("top_ready"), sem("index_ready"), sem("tanh_ready"), sem("picks_ready"), sem("gates_ready")
        gatesT_ps, gatesT_ready = sem("gatesT_ps"), sem("gatesT_ready")
        xc_ready, xcT_ps, xcT_ready = sem("xc_ready"), sem("xcT_ps"), sem("xcT_ready")
        scores_ps, neg_max_ready, probs_ready = sem("scores_ps"), sem("neg_max_ready"), sem("probs_ready")
        probsT_ps, probsT_ready, att_ps, x2_ready = sem("probsT_ps"), sem("probsT_ready"), sem("att_ps"), sem("x2_ready")
        x2n_ready = sem("x2n_ready")
        tokT_ps, tok_hi_ready, tok_ready = sem("tokT_ps"), sem("tok_hi_ready"), sem("tok_ready")
        dve_step = sem("dve_step")
        pool_step = sem("pool_step")
        hi_split, hi_rounded, fc_ready, pj_ready = sem("hi_split"), sem("hi_rounded"), sem("fc_ready"), sem("pj_ready")
        fc_done, gelu_done, hi_cast, lo_done, pj_done = sem("fc_done"), sem("gelu_done"), sem("hi_cast"), sem("lo_done"), sem("pj_done")
        gated_done, acc_added = sem("gated_done"), sem("acc_added")
        y_ps, y_part_ready, y_ready = sem("y_ps"), sem("y_part_ready"), sem("y_ready")

        def half(t, h):
            return t[:, h * BH:(h + 1) * BH, :]

        def some(t, batches):
            return t[:, batches.start:batches.stop, :].rearrange("p b d -> p (b d)")

        def columns(ps, batches):
            return ps[:, 0:len(batches) * P]

        def tokens(t, batches):
            h, first = batches.start // BH, batches.start % BH * P
            return t[:, h, first:first + len(batches) * P]

        def at_least(eng, s, value):
            if not isinstance(value, int) or value > 0:
                eng.wait_ge(s, value)

        block = ctx.enter_context(nc.Block())

        @block.sync
        def _(sp):
            def weights(slot, n):
                sp.dma_start(raw[slot][:, :], w_all[bass.ds(n, 1), :, :].rearrange("n p w -> (n p) w")).then_inc(w_in[slot], 16)

            def gate(slot, e):
                row = gates_dram[bass.ds(e, 1), :]
                sp.dma_start(gate_bc[slot][:, :], row.to_broadcast([P, B * S])).then_inc(gate_in[slot], 16)

            sp.dma_start(half(x_sb, 0), x[0:BH, :, :].rearrange("b p d -> p b d")).then_inc(x_in[0], 16)
            sp.dma_start(small[:, :], per_partition).then_inc(small_in, 16)
            sp.dma_start(half(x_sb, 1), x[BH:B, :, :].rearrange("b p d -> p b d")).then_inc(x_in[1], 16)
            weights(1, 0)
            weights(0, 1)
            sp.wait_ge(pj_ready, 1)
            weights(1, 2)
            sp.wait_ge(pj_ready, 2)
            weights(0, 3)
            for h in range(HALVES):
                cols = slice(h * N, (h + 1) * N)
                sp.wait_ge(gatesT_ready, h + 1)
                sp.dma_start(gates_dram[:, cols], gatesT[:, h, :]).then_inc(gates_stored, 16)
                sp.wait_ge(gates_stored, 16 * (h + 1))
                sp.dma_start(gate_bc[0][:, cols], gates_dram[0:1, cols].to_broadcast([P, N])).then_inc(gate_in[0] if h else gate_first, 16)

            def expert_pair(it, last):
                sp.wait_ge(gated_done, 4 * it + 3)
                gate(1, 2 * it + 1)
                sp.wait_ge(pj_ready, 2 * it + 3)
                weights(1, 2 * it + 4)
                sp.wait_ge(gated_done, 4 * it + 4)
                gate(0, 2 * it + 2)
                if not last:
                    sp.wait_ge(pj_ready, 2 * it + 4)
                    weights(0, 2 * it + 5)

            with sp.Fori(0, LOOPS - 1) as it:
                expert_pair(it, False)
            expert_pair(LOOPS - 1, True)
            sp.wait_ge(gated_done, UNITS - 2)
            gate(1, E - 1)
            for n, (a, b) in enumerate([(0, BH), (BH, BH + BH // 2), (BH + BH // 2, B)]):
                sp.wait_ge(y_ready, n + 1)
                sp.dma_start(out[a:b, :, :].rearrange("b p d -> p b d"), y[:, a:b, :]).then_inc(out_stored, 16)
            sp.wait_ge(out_stored, 16 * 3)

        @block.tensor
        def _(pe):
            def transposes(ps, src, batches, ready):
                for j, b in enumerate(batches):
                    last = nc.tensor.transpose(ps[:, j * P:(j + 1) * P], src[:, b, :], ident[:, :])
                last.then_inc(ready, 1)

            def masked_keys(part):
                n = len(PARTS[part]) * P
                nc.tensor.matmul(ps_scores[part][:, 0:n], ones_row[:, :],
                                 neg_row[:, PARTS[part].start * P:PARTS[part].stop * P], start=True, stop=False)

            def scores(part):
                pe.wait_ge(ctxT_ready, PARTS[part].start // BH + 1)
                pe.wait_ge(xcT_ready, part + 1)
                for j, b in enumerate(PARTS[part]):
                    last = nc.tensor.matmul(ps_scores[part][:, j * P:(j + 1) * P], xcT[:, b, :], ctxT[:, b, :],
                                            start=False, stop=(j == len(PARTS[part]) - 1))
                last.then_inc(scores_ps, 1)

            def probs_transposed(part):
                pe.wait_ge(probs_ready, part + 1)
                transposes(ps_probsT[part], probs, PARTS[part], probsT_ps)

            def attention(part):
                pe.wait_ge(probsT_ready, part + 1)
                pe.wait_ge(v_ready, PARTS[part].start // BH + 1)
                for j, b in enumerate(PARTS[part]):
                    last = nc.tensor.matmul(ps_att[part][:, j * P:(j + 1) * P], probsT[:, b, :], v_masked[:, b, :],
                                            start=True, stop=True)
                last.then_inc(att_ps, 1)

            def tokens_transposed(part):
                pe.wait_ge(x2n_ready, part + 1)
                transposes(ps_tokT[part], x2n, PARTS[part], tokT_ps)

            pe.wait_ge(ident_ready, 1)
            def keep_clock(bank, times):
                for _ in range(times):
                    nc.tensor.matmul(bank[:, 0:P], ident[:, :], ident[:, :], start=True, stop=True)

            keep_clock(ps_h[3], WARM_UP)
            for h in range(HALVES):
                pe.wait_ge(ctx_ld[h], 16)
                transposes(ps_ctxT[h], ctx_sb, range(h * BH, (h + 1) * BH), ctxT_ps)
            pe.wait_ge(ones_ready, 1)
            pe.wait_ge(neg_ready, 1)
            masked_keys(0)
            masked_keys(1)
            for part in range(2):
                pe.wait_ge(xc_ready, part + 1)
                transposes(ps_xcT[part], xc, PARTS[part], xcT_ps)
            scores(0)
            scores(1)
            pe.wait_ge(xc_ready, 3)
            pe.wait_ge(ctxT_ready, 2)
            transposes(ps_xcT[2], xc, PARTS[2], xcT_ps)
            masked_keys(2)
            probs_transposed(0)
            probs_transposed(1)
            attention(0)
            attention(1)
            scores(2)
            keep_clock(ps_h[2], FILL)

            def three_passes(ps, w_hi, w_lo, m_hi, m_lo, start, stop):
                nc.tensor.matmul(ps, w_hi, m_hi, start=start, stop=False)
                nc.tensor.matmul(ps, w_hi, m_lo, start=False, stop=False)
                return nc.tensor.matmul(ps, w_lo, m_hi, start=False, stop=stop)

            def first_product(slot, h, c, g):
                at_least(pe, gelu_done, g - 3)
                cols = slice(c * P, (c + 1) * P)
                three_passes(ps_h[c][:, :], fc_hi[slot][:, cols], fc_lo[slot][:, cols],
                             tok_hi[:, h, :], tok_lo[:, h, :], True, True).then_inc(fc_done, 1)

            def second_product(slot, bank, c, g, r):
                pe.wait_ge(lo_done, g + 1)
                cols = slice(c * P, (c + 1) * P)
                three_passes(ps_o[bank][:, :], pj_hi[slot][:, cols], pj_lo[slot][:, cols],
                             hid_hi[:, r, :], hid_lo[:, r, :], c == 0, c == C - 1).then_inc(pj_done, 1)

            def logits(h):
                for b in range(BH):
                    o = ps_logits[h][:, b, :]
                    cols = slice(b * P, (b + 1) * P)
                    nc.tensor.matmul(o, tok_hi[:, h, cols], wr_parts[:, :], start=True, stop=False)
                    last = nc.tensor.matmul(o[:, 0:E], tok_lo[:, h, cols], wr_parts[:, 0:E], start=False, stop=True)
                last.then_inc(logits_ps, 1)

            def gates_transposed(h):
                pe.wait_ge(gates_ready, h + 1)
                for b in range(BH):
                    last = nc.tensor.transpose(ps_gatesT[h][0:E, b * P:(b + 1) * P], gates[:, h * BH + b, :], ident[:, :])
                last.then_inc(gatesT_ps, 1)

            tokens_transposed(0)
            tokens_transposed(1)
            probs_transposed(2)
            for g in range(PEELED):
                number, h = FIRST_UNITS[g // C]
                if g % C == 0:
                    pe.wait_ge(tok_ready, HALF_PARTS[h])
                    pe.wait_ge(fc_ready, number + 1)
                if g == 0:
                    pe.wait_ge(x2_ready, 2)
                first_product((number + 1) % 2, h, g % C, g)
                if g == 0:
                    attention(2)
                if g == 1:
                    pe.wait_ge(wr_ready, 1)
                    logits(0)
                if g >= LAG:
                    j = g - LAG
                    number = FIRST_UNITS[j // C][0]
                    if j % C == 0:
                        pe.wait_ge(pj_ready, number + 1)
                        pe.wait_ge(x2_ready, 3)
                        at_least(pe, gated_done, j // C - 1)
                    second_product((number + 1) % 2, j // C % 2, j % C, j, j % RING)
                if g == 5:
                    tokens_transposed(2)
                if g == 7:
                    gates_transposed(0)
                if g == 8:
                    logits(1)
                if g == 15:
                    gates_transposed(1)

            def expert_chunks(number, first_k, it, last_k):
                for k in range(first_k, last_k):
                    g = PAIR * it + (PEELED + k)
                    slot, h, c = 1 - k // OF_EXPERT, k // C % HALVES, k % C
                    if k % OF_EXPERT == 0:
                        pe.wait_ge(fc_ready, number + (1 + k // OF_EXPERT))
                    first_product(slot, h, c, g)
                    j = k - LAG
                    if j % OF_EXPERT == 0:
                        pe.wait_ge(pj_ready, number + (1 + j // OF_EXPERT))
                    if j % C == 0:
                        pe.wait_ge(gated_done, 4 * it + (3 + j // C))
                    second_product(1 - j // OF_EXPERT if j >= 0 else 0, j // C % 2, j % C, g - LAG, j % RING)

            with pe.Fori(0, LOOPS) as it:
                expert_chunks(2 * it + 2, 0, it, PAIR)
            expert_chunks(E, 0, LOOPS, OF_EXPERT)
            for g in range(CHUNKS - LAG, CHUNKS):
                second_product(1, 1, g % C, g, g % RING)
            def back(ps, src, cols, done):
                for j in range(cols.start // P, cols.stop // P):
                    last = nc.tensor.transpose(ps[:, j * P:(j + 1) * P], src[:, j * P:(j + 1) * P], ident[:, :])
                last.then_inc(done, 1)

            pe.wait_ge(gatesT_ready, HALVES)
            pe.wait_ge(acc_added, UNITS - 1)
            back(ps_m[1], acc[:, 1, :], slice(0, N), y_ps)
            pe.wait_ge(acc_added, UNITS)
            back(ps_m[0], acc[:, 0, :], slice(0, N), y_ps)
            for j in range(2):
                pe.wait_ge(gated_done, UNITS + j)
                back(ps_h[j], gated[:, 1, :], slice(j * N // 2, (j + 1) * N // 2), y_ps)

        @block.scalar
        def _(act):
            act.dma_start(half(ctx_sb, 0), ctx_in[0:BH, :, :].rearrange("b p d -> p b d")).then_inc(ctx_ld[0], 16)
            act.dma_start(key_words[:, :], key_row).then_inc(key_row_in, 16)
            act.dma_start(half(ctx_sb, 1), ctx_in[BH:B, :, :].rearrange("b p d -> p b d")).then_inc(ctx_ld[1], 16)

            def evacuate(dst, ps, full, done):
                act.wait_ge(full[0], full[1])
                nc.scalar.activation(dst, ps, ACT.Copy).then_inc(done, 1)

            act.wait_ge(warm_ready, 1)
            nc.scalar.activation(warm[:, 1:2], warm[:, 0:1], ACT.Exp)
            act.wait_ge(key_row_in, 16)
            nc.scalar.activation(neg_row[:, :], key_words[:, :].bitcast(U8), ACT.Copy, bias=MASK_NEG,
                                 scale=-MASK_NEG).then_inc(neg_ready, 1)
            for h in range(HALVES):
                evacuate(some(ctxT, range(h * BH, (h + 1) * BH)), ps_ctxT[h][:, :], (ctxT_ps, h + 1), ctxT_ready)
            def scores_operand(part):
                evacuate(some(xcT, PARTS[part]), columns(ps_xcT[part], PARTS[part]), (xcT_ps, part + 1), xcT_ready)

            def exponentials(part):
                act.wait_ge(neg_max_ready, part + 1)
                for j, b in enumerate(PARTS[part]):
                    last = nc.scalar.activation(probs[:, b, :], ps_scores[part][:, j * P:(j + 1) * P], ACT.Exp,
                                                bias=neg_max[:, b:b + 1], scale=exp_scale[:, b:b + 1], accum_out=denom[:, b:b + 1])
                last.then_inc(probs_ready, 1)

            def probs_evacuated(part):
                evacuate(some(probsT, PARTS[part]), columns(ps_probsT[part], PARTS[part]), (probsT_ps, part + 1), probsT_ready)

            scores_operand(0)
            scores_operand(1)
            act.wait_ge(small_in, 16)
            nc.scalar.activation(g_tanh[:, :], g_raw, ACT.Tanh).then_inc(g_ready, 1)
            def weights_rounded(hi, slot, cols):
                act.wait_ge(w_in[slot], 16)
                nc.scalar.activation(hi[slot][:, :], raw[slot][:, cols], ACT.Copy).then_inc(hi_rounded, 1)

            weights_rounded(pj_hi, 1, slice(HID, 2 * HID))
            exponentials(0)
            exponentials(1)
            probs_evacuated(0)
            probs_evacuated(1)
            scores_operand(2)
            weights_rounded(fc_hi, 0, slice(0, HID))
            weights_rounded(pj_hi, 0, slice(HID, 2 * HID))
            exponentials(2)
            nc.scalar.activation(warm[:, 1:2], warm[:, 0:1], ACT.Gelu_apprx_tanh)
            probs_evacuated(2)

            def gelu(slot, c, g, r):
                act.wait_ge(fc_done, g + 1)
                at_least(act, pj_done, g - RING + 1)
                if c % 2 == 0:
                    nc.scalar.activation(hid_hi[:, r, :], ps_h[c][:, :], ACT.Gelu_apprx_tanh, bias=bias[slot][:, c:c + 1])
                nc.scalar.activation(hid[:, r, :], ps_h[c][:, :], ACT.Gelu_apprx_tanh,
                                     bias=bias[slot][:, c:c + 1]).then_inc(gelu_done, 1)

            def gates_evacuated(h):
                evacuate(gatesT[:, h, :], ps_gatesT[h][0:E, :], (gatesT_ps, h + 1), gatesT_ready)

            def top_tanhs(h):
                act.wait_ge(top_ready, h + 1)
                cols = slice(h * BH, (h + 1) * BH)
                nc.scalar.activation(top_tanh[:, cols], top_diff[:, cols], ACT.Tanh, scale=0.5).then_inc(tanh_ready, 1)

            for g in range(PEELED):
                number = FIRST_UNITS[g // C][0]
                gelu((number + 1) % 2, g % C, g, g % RING)
                if g == 3:
                    top_tanhs(0)
                if g == 5:
                    evacuate(tokens(tok_hi, PARTS[2]), columns(ps_tokT[2], PARTS[2]), (tokT_ps, 3), tok_hi_ready)
                if g == 7:
                    gates_evacuated(0)
                if g == 10:
                    top_tanhs(1)
                if g == 15:
                    gates_evacuated(1)

            def expert_chunks(it, last_k):
                for k in range(last_k):
                    gelu(1 - k // OF_EXPERT, k % C, PAIR * it + (PEELED + k), k % RING)

            with act.Fori(0, LOOPS) as it:
                expert_chunks(it, PAIR)
            expert_chunks(LOOPS, OF_EXPERT)

        @block.vector
        def _(dve):
            steps = [0]

            def chain(ins):
                steps[0] += 1
                ins.then_inc(dve_step, 1)
                dve.wait_ge(dve_step, steps[0])

            def variance(src, batches, moments, var, ready):
                for b in batches:
                    last = nc.vector.bn_stats(stats[:, b, :], src[:, b, :])
                chain(last)
                for b in batches:
                    last = nc.vector.bn_aggr(moments[:, b, :], stats[:, b, :])
                chain(last)
                cols = slice(batches.start, batches.stop)
                nc.vector.tensor_scalar(var[:, cols], moments[:, cols, 1], LN_EPS, None, ALU.add).then_inc(ready, 1)

            def centre(batches):
                cols = slice(batches.start, batches.stop)
                nc.vector.tensor_tensor(xc[:, cols, :], x_sb[:, cols, :],
                                        moments1[:, cols, 0:1].to_broadcast([P, len(batches), D]),
                                        ALU.subtract).then_inc(xc_ready, 1)

            def largest_score(part):
                batches = PARTS[part]
                cols = slice(batches.start, batches.stop)
                dve.wait_ge(scores_ps, part + 1)
                chain(nc.vector.reduce_max(smax[:, cols], columns(ps_scores[part], batches).rearrange("p (b k) -> p b k", k=S), AX_X))
                nc.vector.scalar_tensor_tensor(neg_max[:, cols], smax[:, cols], -1.0, exp_scale[:, cols],
                                               ALU.mult, ALU.mult).then_inc(neg_max_ready, 1)

            def row_scales(part):
                cols = slice(PARTS[part].start, PARTS[part].stop)
                dve.wait_ge(probs_ready, part + 1)
                chain(nc.vector.reciprocal(inv_denom[:, cols], denom[:, cols]))
                chain(nc.vector.tensor_tensor(row_scale[:, cols], inv_denom[:, cols], q_scale[:, cols], ALU.mult))

            def residual(part):
                dve.wait_ge(att_ps, part + 1)
                for j, b in enumerate(PARTS[part]):
                    last = nc.vector.scalar_tensor_tensor(x2[:, b, :], ps_att[part][:, j * P:(j + 1) * P],
                                                          row_scale[:, b:b + 1], x_sb[:, b, :], ALU.mult, ALU.add)
                last.then_inc(x2_ready, 1)

            def normalise(part):
                dve.wait_ge(rstd2_ready, 1)
                for b in PARTS[part]:
                    last = nc.vector.tensor_scalar(x2n[:, b, :], x2[:, b, :], moments2[:, b, 0:1], rstd[:, 1, b:b + 1],
                                                   ALU.subtract, ALU.mult)
                last.then_inc(x2n_ready, 1)

            def split_tokens(part):
                if part < 2:
                    dve.wait_ge(tokT_ps, part + 1)
                    nc.vector.tensor_copy(tokens(tok_hi, PARTS[part]), columns(ps_tokT[part], PARTS[part])).then_inc(tok_hi_ready, 1)
                dve.wait_ge(tok_hi_ready, part + 1)
                nc.vector.tensor_tensor(tokens(tok_lo, PARTS[part]), columns(ps_tokT[part], PARTS[part]),
                                        tokens(tok_hi, PARTS[part]).bitcast(F32), ALU.subtract).then_inc(tok_ready, 1)

            nc.vector.memset(warm[:, :], 0.0).then_inc(warm_ready, 1)
            nc.vector.memset(ones_row[:, :], 1.0).then_inc(ones_ready, 1)
            dve.wait_ge(x_in[0], 16)
            variance(x_sb, range(0, BH), moments1, var_eps[:, 0, :], var1_ready)
            centre(PARTS[0])
            centre(PARTS[1])
            dve.wait_ge(small_in, 16)
            nc.vector.tensor_copy(mask_f[:, :], masks_u8).then_inc(mask_f_ready, 1)
            dve.wait_ge(x_in[1], 16)
            variance(x_sb, range(BH, B), moments1, var_eps[:, 0, :], var1_ready)
            dve.wait_ge(rstd1_ready, 1)
            chain(nc.vector.tensor_scalar(exp_scale[:, 0:BH], rstd[:, 0, 0:BH], SCALE, None, ALU.mult))
            centre(PARTS[2])
            largest_score(0)
            largest_score(1)
            dve.wait_ge(rstd1_ready, 2)
            chain(nc.vector.tensor_scalar(exp_scale[:, BH:B], rstd[:, 0, BH:B], SCALE, None, ALU.mult))
            dve.wait_ge(g_ready, 1)
            dve.wait_ge(mask_f_ready, 1)
            chain(nc.vector.tensor_scalar(q_scale[:, :], mask_f[:, 0:B], g_tanh[:, 0:1], None, ALU.mult))
            chain(nc.vector.tensor_copy(wr_parts[:, 0:E], wr_raw))
            nc.vector.tensor_tensor(wr_parts[:, E:2 * E], wr_raw, wr_parts[:, 0:E].bitcast(F32), ALU.subtract).then_inc(wr_ready, 1)
            for part in range(2):
                row_scales(part)
            residual(0)
            residual(1)
            dve.wait_ge(x2_ready, 2)
            variance(x2, range(0, BH), moments2, var_eps[:, 1, :], var2_ready)
            largest_score(2)
            normalise(0)
            normalise(1)
            split_tokens(0)
            split_tokens(1)

            def lower_part(c, g, casts, r):
                dve.wait_ge(gelu_done, g + 1)
                at_least(dve, pj_done, g - RING + 1)
                if c % 2:
                    nc.vector.tensor_copy(hid_hi[:, r, :], hid[:, r, :]).then_inc(hi_cast, 1)
                    dve.wait_ge(hi_cast, casts + 1)
                nc.vector.tensor_tensor(hid_lo[:, r, :], hid[:, r, :], hid_hi[:, r, :].bitcast(F32),
                                        ALU.subtract).then_inc(lo_done, 1)

            def gate_unit(slot, h, u, bank, loads, pieces=1, loaded=None):
                dve.wait_ge(pj_done, 4 * u + 4)
                if loads is not None:
                    dve.wait_ge(loaded or gate_in[slot], loads)
                at_least(dve, acc_added, u)
                for j in range(pieces):
                    cols = slice(j * N // pieces, (j + 1) * N // pieces)
                    nc.vector.scalar_tensor_tensor(gated[:, bank, cols], ps_o[bank][:, cols], bias[slot][:, C:C + 1],
                                                   gate_bc[slot][:, h * N + cols.start:h * N + cols.stop],
                                                   ALU.add, ALU.mult).then_inc(gated_done, 1)

            def top_two(h):
                cols = slice(h * BH, (h + 1) * BH)
                dve.wait_ge(logits_ps, h + 1)
                chain(nc.vector.tensor_copy(half(logits_sb, h), ps_logits[h][:, :, 0:E]))
                chain(nc.vector.tensor_tensor(half(logits_sb, h), half(logits_sb, h), ps_logits[h][:, :, E:2 * E], ALU.add))
                for b in range(h * BH, (h + 1) * BH):
                    last = nc.vector.max(top[:, b, :], logits_sb[:, b, :])
                chain(last)
                nc.vector.tensor_tensor(top_diff[:, cols], top[:, cols, 0], top[:, cols, 1], ALU.subtract).then_inc(top_ready, 1)
                for b in range(h * BH, (h + 1) * BH):
                    last = nc.vector.max_index(top_idx[:, b, :], top[:, b, :], logits_sb[:, b, :])
                chain(last)
                nc.vector.tensor_copy(top_idx_f[:, cols, :], top_idx[:, cols, 0:2]).then_inc(index_ready, 1)

            dve.wait_ge(consts_ready, 1)
            for g in range(PEELED):
                lower_part(g % C, g, g // 2, g % RING)
                if g == 0:
                    row_scales(2)
                    residual(2)
                    dve.wait_ge(x2_ready, 3)
                    variance(x2, PARTS[2], moments2, var_eps[:, 1, :], var2_ready)
                if g == 2:
                    top_two(0)
                if g == 6:
                    split_tokens(2)
                    gate_unit(1, 0, 0, 0, None)
                if g == 9:
                    top_two(1)
                if g == 12:
                    gate_unit(0, 0, 1, 1, 16, loaded=gate_first)
                if g == 14:
                    gate_unit(1, 1, 2, 0, None)

            def expert_chunks(it, last_k):
                for k in range(last_k):
                    lower_part(k % C, PAIR * it + (PEELED + k), PAIR // 2 * it + (PEELED + k) // 2, k % RING)
                    if k % C == 2:
                        j = k - (C + 2)
                        slot, h = (1 - j // OF_EXPERT, j // C % HALVES) if j >= 0 else (0, 1)
                        loads = 16 * it + (32 if j >= 0 and slot == 0 else 16)
                        gate_unit(slot, h, 4 * it + (4 + j // C), h, loads)

            with dve.Fori(0, LOOPS) as it:
                expert_chunks(it, PAIR)
            expert_chunks(LOOPS, OF_EXPERT)
            half_1 = range(BH, B)
            dve.wait_ge(y_ps, 1)
            nc.vector.scalar_tensor_tensor(some(y, half_1), ps_m[1][:, :], g_tanh[:, 1:2], some(x2, half_1),
                                           ALU.mult, ALU.add).then_inc(y_part_ready, 1)
            gate_unit(1, 1, UNITS - 1, 1, 16 * (LOOPS + 1), pieces=2)
            dve.wait_ge(y_ps, 2)
            nc.vector.scalar_tensor_tensor(some(y, range(0, BH)), ps_m[0][:, :], g_tanh[:, 1:2], some(x2, range(0, BH)),
                                           ALU.mult, ALU.add).then_inc(y_ready, 1)
            dve.wait_ge(y_part_ready, 1)
            for j in range(2):
                batches = range(BH + j * BH // 2, BH + (j + 1) * BH // 2)
                dve.wait_ge(y_ps, 3 + j)
                nc.vector.scalar_tensor_tensor(some(y, batches), ps_h[j][:, j * N // 2:(j + 1) * N // 2], g_tanh[:, 1:2],
                                               some(y, batches), ALU.mult, ALU.add).then_inc(y_ready, 1)

        @block.gpsimd
        def _(pool):
            nc.gpsimd.memset(ident[:, :], 0.0).then_inc(ident_zero, 1)
            pool.wait_ge(ident_zero, 1)
            nc.gpsimd.affine_select(out=ident[:, :], in_=ident[:, :], compare_op=ALU.not_equal, fill=1.0,
                                    base=0, pattern=[[-1, P]], channel_multiplier=1).then_inc(ident_ready, 1)
            nc.gpsimd.memset(minus_half[:, :], -0.5).then_inc(ident_zero, 1)
            pool.wait_ge(ident_zero, 2)

            for h in range(HALVES):
                last = nc.gpsimd.memset(acc[:, h, :], 0.0)
            last.then_inc(acc_added, 1)
            nc.gpsimd.memset(gate_bc[1][:, :], 1.0)
            for e in range(E):
                last = nc.gpsimd.memset(expert_id[:, e:e + 1], float(e))
            last.then_inc(consts_ready, 1)

            steps = [0]

            def chain(ins):
                steps[0] += 1
                ins.then_inc(pool_step, 1)
                pool.wait_ge(pool_step, steps[0])

            def inverse_std(k, batches, var_ready, count, ready):
                cols = slice(batches.start, batches.stop)
                pool.wait_ge(var_ready, count)
                return nc.gpsimd.tensor_tensor(rstd[:, k, cols], var_eps[:, k, cols], minus_half[:, 0:len(batches)],
                                               ALU.pow).then_inc(ready, 1)

            def masked_values(h):
                cols = slice(h * BH, (h + 1) * BH)
                pool.wait_ge(mask_f_ready, 1)
                pool.wait_ge(ctx_ld[h], 16)
                nc.gpsimd.tensor_tensor(v_masked[:, cols, :], ctx_sb[:, cols, :],
                                        mask_f[:, B + h * BH:B + (h + 1) * BH].rearrange("p (b o) -> p b o", o=1).to_broadcast([P, BH, D]),
                                        ALU.mult).then_inc(v_ready, 1)

            inverse_std(0, range(0, BH), var1_ready, 1, rstd1_ready)
            masked_values(0)
            inverse_std(0, range(BH, B), var1_ready, 2, rstd1_ready)
            def split(hi, lo, src, number, rounded):
                if rounded:
                    pool.wait_ge(hi_rounded, rounded)
                else:
                    nc.gpsimd.tensor_scalar(hi[:, :], src, 1.0, 1.0, ALU.mult, ALU.mult).then_inc(hi_split, 1)
                    pool.wait_ge(hi_split, number)
                return nc.gpsimd.tensor_tensor(lo[:, :], src, hi[:, :].bitcast(F32), ALU.subtract)

            def split_fc(slot, loads, n, rounded=0):
                pool.wait_ge(w_in[slot], loads)
                nc.gpsimd.tensor_copy(bias[slot][:, 0:C], biasT[:, bass.ds((C + 1) * n, C)])
                number = 2 * n - 2 if not isinstance(n, int) or n else 1
                split(fc_hi[slot], fc_lo[slot], raw[slot][:, 0:HID], number, rounded).then_inc(fc_ready, 1)

            def split_pj(slot, n, rounded=0):
                nc.gpsimd.tensor_copy(bias[slot][:, C:C + 1], biasT[:, bass.ds((C + 1) * n + C, 1)])
                split(pj_hi[slot], pj_lo[slot], raw[slot][:, HID:2 * HID], 2 * n - 1, rounded).then_inc(pj_ready, 1)

            def add_unit(h, u, bank):
                pool.wait_ge(gated_done, u + 1)
                pool.wait_ge(acc_added, u + 1)
                nc.gpsimd.tensor_tensor(acc[:, h, :], acc[:, h, :], gated[:, bank, :], ALU.add).then_inc(acc_added, 1)

            def normalise(part):
                batches = PARTS[part]
                cols = slice(batches.start, batches.stop)
                inverse_std(1, batches, var2_ready, 2, rstd2_ready)
                chain(nc.gpsimd.tensor_scalar(minus_mean[:, :], moments2[:, cols, 0], -1.0, 1.0, ALU.mult, ALU.mult))
                pool.wait_ge(rstd2_ready, 2)
                for j, b in enumerate(batches):
                    last = nc.gpsimd.tensor_scalar(x2n[:, b, :], x2[:, b, :], minus_mean[:, j:j + 1], rstd[:, 1, b:b + 1],
                                                   ALU.add, ALU.mult)
                last.then_inc(x2n_ready, 1)

            def route(h):
                cols = slice(h * BH, (h + 1) * BH)
                pool.wait_ge(tanh_ready, h + 1)
                pool.wait_ge(index_ready, h + 1)
                nc.gpsimd.tensor_scalar(gate_top[:, 0, cols], top_tanh[:, cols], 0.5, 0.5, ALU.mult, ALU.add)
                chain(nc.gpsimd.tensor_scalar(gate_top[:, 1, cols], top_tanh[:, cols], -0.5, 0.5, ALU.mult, ALU.add))
                for b in range(h * BH, (h + 1) * BH):
                    for k, pick in enumerate((pick1, pick2)):
                        last = nc.gpsimd.tensor_scalar(pick[:, b, :], expert_id[:, :], top_idx_f[:, b, k:k + 1],
                                                       gate_top[:, k, b:b + 1], ALU.is_equal, ALU.mult)
                chain(last)
                nc.gpsimd.tensor_tensor(half(gates, h), half(pick1, h), half(pick2, h), ALU.add).then_inc(gates_ready, 1)

            pool.wait_ge(small_in, 16)
            split_fc(1, 16, 0)
            masked_values(1)
            split_pj(1, 0, rounded=1)
            inverse_std(1, range(0, BH), var2_ready, 1, rstd2_ready)
            split_fc(0, 16, 1, rounded=2)
            split_pj(0, 1, rounded=3)
            normalise(2)
            route(0)
            add_unit(0, 0, 0)
            route(1)
            pool.wait_ge(fc_done, 3 * C)
            pool.wait_ge(gelu_done, 3 * C)
            split_fc(1, 32, 2)
            add_unit(0, 1, 1)
            add_unit(1, 2, 0)
            pool.wait_ge(pj_done, 3 * C)
            split_pj(1, 2)
            pool.wait_ge(fc_done, 4 * C)
            pool.wait_ge(gelu_done, 4 * C)
            split_fc(0, 32, 3)
            add_unit(1, 3, 1)
            pool.wait_ge(pj_done, 4 * C)
            split_pj(0, 3)

            def expert_pair(it, last):
                add_unit(0, 4 * it + 4, 0)
                pool.wait_ge(fc_done, PAIR * it + (PEELED + OF_EXPERT))
                pool.wait_ge(gelu_done, PAIR * it + (PEELED + OF_EXPERT))
                split_fc(1, 16 * it + 48, 2 * it + 4)
                add_unit(1, 4 * it + 5, 1)
                pool.wait_ge(pj_done, PAIR * it + (PEELED + OF_EXPERT))
                split_pj(1, 2 * it + 4)
                add_unit(0, 4 * it + 6, 0)
                if not last:
                    pool.wait_ge(fc_done, PAIR * it + (PEELED + PAIR))
                    pool.wait_ge(gelu_done, PAIR * it + (PEELED + PAIR))
                    split_fc(0, 16 * it + 48, 2 * it + 5)
                add_unit(1, 4 * it + 7, 1)
                if not last:
                    pool.wait_ge(pj_done, PAIR * it + (PEELED + PAIR))
                    split_pj(0, 2 * it + 5)

            with pool.Fori(0, LOOPS - 1) as it:
                expert_pair(it, False)
            expert_pair(LOOPS - 1, True)
            add_unit(0, UNITS - 2, 0)


def kernel(x, ctx_1024, mask_BxS2_bk1, mask_BxS2_bk0, g_xattn, g_ffn, L0_ffn_Wfc_s, L0_ffn_bfc_s, L0_ffn_Wproj_s,
           L0_ffn_bproj_s, L0_ffn_Wr, L0_ffn_Wfc, L0_ffn_bfc, L0_ffn_Wproj, L0_ffn_bproj):
    import numpy as np
    import concourse.bacc as bacc
    from concourse.bass_utils import run_bass_kernel_spmd

    P = 128
    q_mask, k_mask = np.asarray(mask_BxS2_bk1), np.asarray(mask_BxS2_bk0)
    w_fc = np.concatenate([np.asarray(L0_ffn_Wfc_s)[None], np.asarray(L0_ffn_Wfc)])
    w_pj = np.concatenate([np.asarray(L0_ffn_Wproj_s)[None], np.asarray(L0_ffn_Wproj)])
    b_fc = np.concatenate([np.asarray(L0_ffn_bfc_s)[None], np.asarray(L0_ffn_bfc)])
    b_pj = np.concatenate([np.asarray(L0_ffn_bproj_s)[None], np.asarray(L0_ffn_bproj)])
    n, hid, d = w_pj.shape
    w_pj = w_pj.reshape(n, hid // P, P, d).transpose(0, 2, 1, 3).reshape(n, P, hid)
    bias_cols = np.concatenate([b_fc.reshape(n, hid // P, P), b_pj[:, None, :]], axis=1).transpose(2, 0, 1)
    words = np.uint32
    per_partition = np.concatenate([
        np.ascontiguousarray(np.concatenate([q_mask, k_mask]).T).view(words),
        np.ascontiguousarray(bias_cols).reshape(P, -1).view(words),
        np.ascontiguousarray(L0_ffn_Wr).view(words),
        np.tile(np.concatenate([np.asarray(g_xattn), np.asarray(g_ffn)]), (P, 1)).view(words),
    ], axis=1)
    arrays = {
        "x": np.ascontiguousarray(x),
        "ctx_in": np.ascontiguousarray(ctx_1024),
        "key_row": np.ascontiguousarray(k_mask).reshape(1, -1).view(words),
        "per_partition": per_partition,
        "w_all": np.ascontiguousarray(np.concatenate([w_fc, w_pj], axis=2)),
    }
    nc = bacc.Bacc("TRN2", target_bir_lowering=False, num_devices=1)
    args = [nc.dram_tensor(f"in_{name}", a.shape, mybir.dt.from_np(a.dtype), kind="ExternalInput").ap()
            for name, a in arrays.items()]
    out = nc.dram_tensor("out_0", arrays["x"].shape, F32, kind="ExternalOutput").ap()
    flamingo_gated_moe(nc, *args, out)
    r = run_bass_kernel_spmd(nc, [{f"in_{name}": a for name, a in arrays.items()}], core_ids=[0])
    return r.results[0]["out_0"]
```

```python
from contextlib import ExitStack

import concourse.bass as bass
from concourse import mybir

F32 = mybir.dt.float32
F32R = mybir.dt.float32r
BF16 = mybir.dt.bfloat16
U8 = mybir.dt.uint8
U32 = mybir.dt.uint32
ALU = mybir.AluOpType
ACT = mybir.ActivationFunctionType
AX_X = mybir.AxisListType.X

LN_EPS = 1e-5
MASK_NEG = -(2.0 ** 100)
RING = 8
LAG = 3
ACT_ROUNDS = 8
WARM_UP = 7
FILL = 8


def flamingo_gated_moe(nc, x, ctx_in, key_row, per_partition, w_all, out):
    B, S, D = x.shape
    E = w_all.shape[0] - 1
    EXPERTS = E + 1
    P = 128
    HID = w_all.shape[2] // 2
    HALVES = 2
    BH = B // HALVES
    N = BH * S
    C = HID // P
    OF_EXPERT = HALVES * C
    PAIR = 2 * OF_EXPERT
    PEELED = PAIR
    LOOPS = (E - 2) // 2
    CHUNKS = OF_EXPERT * EXPERTS
    UNITS = HALVES * EXPERTS
    FIRST_UNITS = [(0, 0), (1, 0), (0, 1), (1, 1)]
    SCALE = float(D) ** -0.5
    PARTS = [range(0, BH // 2), range(BH // 2, BH), range(BH, B)]
    HALF_PARTS = [2, 3]
    PIECES = [slice(0, N // 2), slice(N // 2, N)]
    assert S == P and D == P and N == 512 and E % 2 == 0 and C == 4

    gates_dram = nc.dram_tensor("gates_scratch", (E, B * S), F32, kind="Internal").ap()

    with ExitStack() as ctx:
        def sb(name, shape, dt=F32):
            return ctx.enter_context(nc.sbuf_tensor(name, shape, dt))

        def sem(name):
            return ctx.enter_context(nc.semaphore(name))

        x_sb = sb("x_sb", [P, B, D])
        ctx_sb = sb("ctx_sb", [P, B, D])
        xc = sb("xc", [P, B, D])
        ctxT = sb("ctxT", [P, B, S])
        xcT = sb("xcT", [P, B, S])
        v_masked = sb("v_masked", [P, B, D])
        probs = sb("probs", [P, B, S])
        probsT = sb("probsT", [P, B, S])
        x2 = sb("x2", [P, B, D])
        x2n = sb("x2n", [P, B, D])
        tok_hi = sb("tok_hi", [P, HALVES, N], F32R)
        tok_lo = sb("tok_lo", [P, HALVES, N], F32R)
        stats = sb("stats", [P, B, 6])
        moments1 = sb("moments1", [P, B, 2])
        moments2 = sb("moments2", [P, B, 2])
        var_eps = sb("var_eps", [P, 2, B])
        rstd = sb("rstd", [P, 2, B])
        minus_mean = sb("minus_mean", [P, BH])
        minus_half = sb("minus_half", [P, BH])
        exp_scale = sb("exp_scale", [P, B])
        warm = sb("warm", [P, 2])
        smax = sb("smax", [P, B])
        neg_max = sb("neg_max", [P, B])
        denom = sb("denom", [P, B])
        inv_denom = sb("inv_denom", [P, B])
        row_scale = sb("row_scale", [P, B])
        ident = sb("ident", [P, P])
        ones_row = sb("ones_row", [1, P], BF16)
        MASK_W = 2 * B // 4
        BIAS_W = (E + 1) * (C + 1)
        small = sb("small", [P, MASK_W + BIAS_W + E + 2], U32)
        masks_u8 = small[:, 0:MASK_W].bitcast(U8)
        biasT = small[:, MASK_W:MASK_W + BIAS_W].bitcast(F32)
        wr_raw = small[:, MASK_W + BIAS_W:MASK_W + BIAS_W + E].bitcast(F32)
        g_raw = small[:, MASK_W + BIAS_W + E:MASK_W + BIAS_W + E + 2].bitcast(F32)
        mask_f = sb("mask_f", [P, 2 * B])
        key_words = sb("key_words", [1, B * S // 4], U32)
        neg_row = sb("neg_row", [1, B * S], BF16)
        q_scale = sb("q_scale", [P, B])
        g_tanh = sb("g_tanh", [P, 2])
        wr_parts = sb("wr_parts", [P, 2 * E], F32R)
        top = sb("top", [P, B, 8])
        top_idx = sb("top_idx", [P, B, 8], U32)
        top_idx_f = sb("top_idx_f", [P, 2, B])
        logits_sb = sb("logits_sb", [P, B, E])
        top_diff = sb("top_diff", [P, B])
        top_tanh = sb("top_tanh", [P, B])
        gate_top = sb("gate_top", [P, 2, B])
        expert_id = sb("expert_id", [P, E])
        picks = sb("picks", [P, 2, B, E])
        gates = sb("gates", [P, B, E])
        gatesT = sb("gatesT", [BH * E, HALVES, P])
        raw = [sb(f"raw{s}", [P, 2 * HID]) for s in range(2)]
        fc_hi = [sb(f"fc_hi{s}", [P, HID], F32R) for s in range(2)]
        fc_lo = [sb(f"fc_lo{s}", [P, HID], F32R) for s in range(2)]
        pj_hi = [sb(f"pj_hi{s}", [P, HID], F32R) for s in range(2)]
        pj_lo = [sb(f"pj_lo{s}", [P, HID], F32R) for s in range(2)]
        bias = [sb(f"bias{s}", [P, C + 1]) for s in range(2)]
        gate_bc = [sb(f"gate_bc{s}", [P, HALVES * N]) for s in range(2)]
        hid = sb("hid", [P, RING, N])
        hid_hi = sb("hid_hi", [P, RING, N], F32R)
        hid_lo = sb("hid_lo", [P, RING, N], F32R)
        gated = sb("gated", [P, HALVES, N])
        acc = sb("acc", [P, HALVES, N])
        y = sb("y", [P, B, D])

        ps_h = [ctx.enter_context(nc.psum_tensor(f"ps_h{i}", [P, N], F32)) for i in range(4)]
        ps_o = [ctx.enter_context(nc.psum_tensor(f"ps_o{i}", [P, N], F32)) for i in range(HALVES)]
        ps_m = [ctx.enter_context(nc.psum_tensor(f"ps_m{i}", [P, N], F32)) for i in range(2)]
        ps_ctxT = [ps_m[0], ps_m[1]]
        ps_xcT = [ps_h[0], ps_h[1], ps_m[0]]
        ps_scores = [ps_o[0], ps_o[1], ps_m[1]]
        ps_probsT = [ps_h[2], ps_h[3], ps_o[0]]
        ps_att = [ps_h[0], ps_h[1], ps_o[1]]
        ps_tokT = [ps_h[2], ps_m[0], ps_m[0]]
        ps_logits = [ps_m[i][:, 0:BH * 2 * E].rearrange("p (b e) -> p b e", b=BH) for i in (1, 0)]
        ps_gatesT = [ps_m[1], ps_m[0]]

        x_in = [sem(f"x_in{h}") for h in range(HALVES)]
        ctx_ld = [sem(f"ctx_ld{h}") for h in range(HALVES)]
        key_row_in, small_in = sem("key_row_in"), sem("small_in")
        w_in = [sem(f"w_in{s}") for s in range(2)]
        gate_first = sem("gate_first")
        gate_in = [sem(f"gate_in{s}") for s in range(2)]
        gates_stored = sem("gates_stored")
        out_stored = sem("out_stored")
        ident_zero, ident_ready, consts_ready = sem("ident_zero"), sem("ident_ready"), sem("consts_ready")
        ones_ready, mask_f_ready, neg_ready, warm_ready = sem("ones_ready"), sem("mask_f_ready"), sem("neg_ready"), sem("warm_ready")
        g_ready, wr_ready = sem("g_ready"), sem("wr_ready")
        var1_ready, rstd1_ready = sem("var1_ready"), sem("rstd1_ready")
        ctxT_ps, ctxT_ready, v_ready = sem("ctxT_ps"), sem("ctxT_ready"), sem("v_ready")
        logits_ps, top_ready, index_ready, tanh_ready, gates_ready = sem("logits_ps"), sem("top_ready"), sem("index_ready"), sem("tanh_ready"), sem("gates_ready")
        gatesT_ps, gatesT_ready = sem("gatesT_ps"), sem("gatesT_ready")
        xc_ready, xcT_ps, xcT_ready = sem("xc_ready"), sem("xcT_ps"), sem("xcT_ready")
        scores_ps, neg_max_ready, probs_ready = sem("scores_ps"), sem("neg_max_ready"), sem("probs_ready")
        probsT_ps, probsT_ready, att_ps, x2_ready = sem("probsT_ps"), sem("probsT_ready"), sem("att_ps"), sem("x2_ready")
        var2_ready, rstd2_ready, x2n_ready = sem("var2_ready"), sem("rstd2_ready"), sem("x2n_ready")
        tokT_ps, tok_hi_ready, tok_ready = sem("tokT_ps"), sem("tok_hi_ready"), sem("tok_ready")
        stats_ready = sem("stats_ready")
        dve_step = sem("dve_step")
        pool_step = sem("pool_step")
        hi_split, hi_rounded, fc_ready, pj_ready = sem("hi_split"), sem("hi_rounded"), sem("fc_ready"), sem("pj_ready")
        fc_done, gelu_done, hi_cast, lo_done, pj_done = sem("fc_done"), sem("gelu_done"), sem("hi_cast"), sem("lo_done"), sem("pj_done")
        gated_done, acc_added = sem("gated_done"), sem("acc_added")
        last_done, sum_scaled = sem("last_done"), sem("sum_scaled")
        y_ps, y_part_ready, y_ready = sem("y_ps"), sem("y_part_ready"), sem("y_ready")

        def half(t, h):
            return t[:, h * BH:(h + 1) * BH, :]

        def some(t, batches):
            return t[:, batches.start:batches.stop, :].rearrange("p b d -> p (b d)")

        def columns(ps, batches):
            return ps[:, 0:len(batches) * P]

        def tokens(t, batches):
            h, first = batches.start // BH, batches.start % BH * P
            return t[:, h, first:first + len(batches) * P]

        def experts_of(t):
            return t.to_broadcast([P, 2, BH, E])

        def at_least(eng, s, value):
            if not isinstance(value, int) or value > 0:
                eng.wait_ge(s, value)

        block = ctx.enter_context(nc.Block())

        @block.sync
        def _(sp):
            def weights(slot, n):
                sp.dma_start(raw[slot][:, :], w_all[bass.ds(n, 1), :, :].rearrange("n p w -> (n p) w")).then_inc(w_in[slot], 16)

            def gate(slot, e):
                row = gates_dram[bass.ds(e, 1), :]
                sp.dma_start(gate_bc[slot][:, :], row.to_broadcast([P, B * S])).then_inc(gate_in[slot], 16)

            sp.dma_start(half(x_sb, 0), x[0:BH, :, :].rearrange("b p d -> p b d")).then_inc(x_in[0], 16)
            sp.dma_start(small[:, :], per_partition).then_inc(small_in, 16)
            sp.dma_start(half(x_sb, 1), x[BH:B, :, :].rearrange("b p d -> p b d")).then_inc(x_in[1], 16)
            weights(1, 0)
            weights(0, 1)
            sp.wait_ge(pj_ready, 1)
            weights(1, 2)
            sp.wait_ge(pj_ready, 2)
            weights(0, 3)
            for h in range(HALVES):
                cols = slice(h * N, (h + 1) * N)
                sp.wait_ge(gatesT_ready, h + 1)
                sp.dma_start(gates_dram[:, cols].rearrange("e (b t) -> b e t", b=BH), gatesT[:, h, :]).then_inc(gates_stored, 16)
                sp.wait_ge(gates_stored, 16 * (h + 1))
                sp.dma_start(gate_bc[0][:, cols], gates_dram[0:1, cols].to_broadcast([P, N])).then_inc(gate_in[0] if h else gate_first, 16)

            def expert_pair(it, last):
                sp.wait_ge(gated_done, 4 * it + 3)
                gate(1, 2 * it + 1)
                sp.wait_ge(pj_ready, 2 * it + 3)
                weights(1, 2 * it + 4)
                sp.wait_ge(gated_done, 4 * it + 4)
                gate(0, 2 * it + 2)
                if not last:
                    sp.wait_ge(pj_ready, 2 * it + 4)
                    weights(0, 2 * it + 5)

            with sp.Fori(0, LOOPS - 1) as it:
                expert_pair(it, False)
            expert_pair(LOOPS - 1, True)
            sp.wait_ge(gated_done, UNITS - 2)
            gate(1, E - 1)
            for n, (a, b) in enumerate([(0, BH), (BH, BH + BH // 2), (BH + BH // 2, B)]):
                sp.wait_ge(y_ready, n + 1)
                sp.dma_start(out[a:b, :, :].rearrange("b p d -> p b d"), y[:, a:b, :]).then_inc(out_stored, 16)
            sp.wait_ge(out_stored, 16 * 3)

        @block.tensor
        def _(pe):
            def transposes(ps, src, batches, ready):
                for j, b in enumerate(batches):
                    last = nc.tensor.transpose(ps[:, j * P:(j + 1) * P], src[:, b, :], ident[:, :])
                last.then_inc(ready, 1)

            def masked_keys(part):
                n = len(PARTS[part]) * P
                nc.tensor.matmul(ps_scores[part][:, 0:n], ones_row[:, :],
                                 neg_row[:, PARTS[part].start * P:PARTS[part].stop * P], start=True, stop=False)

            def scores(part):
                pe.wait_ge(ctxT_ready, PARTS[part].start // BH + 1)
                pe.wait_ge(xcT_ready, part + 1)
                for j, b in enumerate(PARTS[part]):
                    last = nc.tensor.matmul(ps_scores[part][:, j * P:(j + 1) * P], xcT[:, b, :], ctxT[:, b, :],
                                            start=False, stop=(j == len(PARTS[part]) - 1))
                last.then_inc(scores_ps, 1)

            def probs_transposed(part):
                pe.wait_ge(probs_ready, part + 1)
                transposes(ps_probsT[part], probs, PARTS[part], probsT_ps)

            def attention(part):
                pe.wait_ge(probsT_ready, part + 1)
                pe.wait_ge(v_ready, PARTS[part].start // BH + 1)
                for j, b in enumerate(PARTS[part]):
                    last = nc.tensor.matmul(ps_att[part][:, j * P:(j + 1) * P], probsT[:, b, :], v_masked[:, b, :],
                                            start=True, stop=True)
                last.then_inc(att_ps, 1)

            def tokens_transposed(part):
                pe.wait_ge(x2n_ready, part + 1)
                transposes(ps_tokT[part], x2n, PARTS[part], tokT_ps)

            def context_transposed(h):
                pe.wait_ge(ctx_ld[h], 16)
                transposes(ps_ctxT[h], ctx_sb, range(h * BH, (h + 1) * BH), ctxT_ps)

            def centred_transposed(part):
                pe.wait_ge(xc_ready, part + 1)
                transposes(ps_xcT[part], xc, PARTS[part], xcT_ps)

            def keep_clock(bank, times):
                for _ in range(times):
                    nc.tensor.matmul(bank[:, 0:P], ident[:, :], ident[:, :], start=True, stop=True)

            pe.wait_ge(ident_ready, 1)
            keep_clock(ps_h[3], WARM_UP)
            context_transposed(0)
            centred_transposed(0)
            centred_transposed(1)
            pe.wait_ge(ones_ready, 1)
            pe.wait_ge(neg_ready, 1)
            masked_keys(0)
            scores(0)
            masked_keys(1)
            scores(1)
            context_transposed(1)
            probs_transposed(0)
            centred_transposed(2)
            attention(0)
            probs_transposed(1)
            pe.wait_ge(ctxT_ready, 2)
            masked_keys(2)
            attention(1)
            scores(2)
            keep_clock(ps_h[2], FILL)

            def three_passes(ps, w_hi, w_lo, m_hi, m_lo, start, stop):
                nc.tensor.matmul(ps, w_hi, m_hi, start=start, stop=False)
                nc.tensor.matmul(ps, w_hi, m_lo, start=False, stop=False)
                return nc.tensor.matmul(ps, w_lo, m_hi, start=False, stop=stop)

            def first_product(slot, h, c, g):
                at_least(pe, gelu_done, g - 3)
                cols = slice(c * P, (c + 1) * P)
                three_passes(ps_h[c][:, :], fc_hi[slot][:, cols], fc_lo[slot][:, cols],
                             tok_hi[:, h, :], tok_lo[:, h, :], True, True).then_inc(fc_done, 1)

            def part_product(c, tokens_of):
                cols = slice(c * P, (c + 1) * P)
                return three_passes(ps_h[c][:, tokens_of], fc_hi[1][:, cols], fc_lo[1][:, cols],
                                    tok_hi[:, 0, tokens_of], tok_lo[:, 0, tokens_of], True, True)

            def second_product(slot, bank, c, g, r):
                pe.wait_ge(lo_done, g + 1)
                cols = slice(c * P, (c + 1) * P)
                three_passes(ps_o[bank][:, :], pj_hi[slot][:, cols], pj_lo[slot][:, cols],
                             hid_hi[:, r, :], hid_lo[:, r, :], c == 0, c == C - 1).then_inc(pj_done, 1)

            def logits(h):
                for b in range(BH):
                    o = ps_logits[h][:, b, :]
                    cols = slice(b * P, (b + 1) * P)
                    nc.tensor.matmul(o, tok_hi[:, h, cols], wr_parts[:, :], start=True, stop=False)
                    last = nc.tensor.matmul(o[:, 0:E], tok_lo[:, h, cols], wr_parts[:, 0:E], start=False, stop=True)
                last.then_inc(logits_ps, 1)

            def gates_transposed(h):
                pe.wait_ge(gates_ready, h + 1)
                nc.tensor.transpose(ps_gatesT[h][0:BH * E, 0:P], half(gates, h).rearrange("p b e -> p (b e)"),
                                    ident[:, :]).then_inc(gatesT_ps, 1)

            def second_products(g):
                if g < OF_EXPERT:
                    return range(max(g - LAG - 1, 0), max(g - LAG, 0))
                return range(g - LAG - (g == OF_EXPERT), g - LAG + 1)

            tokens_transposed(0)
            probs_transposed(2)
            for g in range(PEELED):
                number, h = FIRST_UNITS[g // C]
                if g == 0:
                    pe.wait_ge(fc_ready, 1)
                    pe.wait_ge(x2_ready, 2)
                    for part in range(2):
                        pe.wait_ge(tok_ready, part + 1)
                        for c in range(C):
                            if part == 0 and c == C // 2:
                                tokens_transposed(1)
                            last = part_product(c, slice(part * N // 2, (part + 1) * N // 2))
                            if part:
                                last.then_inc(fc_done, 1)
                        if part == 0:
                            attention(2)
                elif g % C == 0:
                    pe.wait_ge(tok_ready, HALF_PARTS[h])
                    pe.wait_ge(fc_ready, number + 1)
                if g >= C:
                    first_product((number + 1) % 2, h, g % C, g)
                if g == 1:
                    pe.wait_ge(wr_ready, 1)
                    logits(0)
                for j in second_products(g):
                    number = FIRST_UNITS[j // C][0]
                    if j % C == 0:
                        pe.wait_ge(pj_ready, number + 1)
                        if j // C == 1:
                            pe.wait_ge(x2_ready, 3)
                        at_least(pe, gated_done, j // C - 1)
                    second_product((number + 1) % 2, j // C % 2, j % C, j, j % RING)
                if g == 6:
                    tokens_transposed(2)
                if g == 7:
                    gates_transposed(0)
                if g == 8:
                    logits(1)
                if g == 13:
                    gates_transposed(1)

            def transposed_back(ps, h, added):
                pe.wait_ge(acc_added, added)
                for j in range(BH):
                    last = nc.tensor.transpose(ps[:, j * P:(j + 1) * P], acc[:, h, j * P:(j + 1) * P], ident[:, :])
                last.then_inc(y_ps, 1)

            def expert_chunks(number, it, ks):
                for k in ks:
                    g = PAIR * it + (PEELED + k)
                    slot, h, c = 1 - k // OF_EXPERT, k // C % HALVES, k % C
                    if k % OF_EXPERT == 0:
                        pe.wait_ge(fc_ready, number + (1 + k // OF_EXPERT))
                    first_product(slot, h, c, g)
                    j = k - LAG
                    if j % OF_EXPERT == 0:
                        pe.wait_ge(pj_ready, number + (1 + j // OF_EXPERT))
                    if j % C == 0:
                        pe.wait_ge(gated_done, 4 * it + (3 + j // C))
                    second_product(1 - j // OF_EXPERT if j >= 0 else 0, j // C % 2, j % C, g - LAG, j % RING)

            with pe.Fori(0, LOOPS) as it:
                expert_chunks(2 * it + 2, it, range(PAIR))
            expert_chunks(E, LOOPS, range(OF_EXPERT - 2))
            pe.wait_ge(gatesT_ready, HALVES)
            transposed_back(ps_m[1], 1, UNITS - 1)
            expert_chunks(E, LOOPS, range(OF_EXPERT - 2, OF_EXPERT - 1))
            first_product(1, 1, C - 1, CHUNKS - 1)

            def last_unit(c, piece, lower_parts):
                pe.wait_ge(lo_done, lower_parts)
                cols, r = slice(c * P, (c + 1) * P), (CHUNKS - C + c) % RING
                return three_passes(ps_o[1 - piece][:, PIECES[piece]], pj_hi[1][:, cols], pj_lo[1][:, cols],
                                    hid_hi[:, r, PIECES[piece]], hid_lo[:, r, PIECES[piece]], c == 0, c == C - 1)

            pe.wait_ge(gated_done, UNITS - 2)
            last_unit(0, 0, CHUNKS - 3)
            last_unit(1, 0, CHUNKS - 2)
            pe.wait_ge(gated_done, UNITS - 1)
            last_unit(0, 1, CHUNKS - 2)
            last_unit(2, 0, CHUNKS - 1)
            last_unit(1, 1, CHUNKS - 2)
            last_unit(3, 0, CHUNKS).then_inc(last_done, 1)
            transposed_back(ps_m[0], 0, UNITS)
            last_unit(2, 1, CHUNKS - 1)
            last_unit(3, 1, CHUNKS + 1).then_inc(last_done, 1)
            for n, piece in enumerate(PIECES):
                pe.wait_ge(gated_done, UNITS + n)
                for j in range(piece.start // P, piece.stop // P):
                    last = nc.tensor.transpose(ps_h[n][:, j * P:(j + 1) * P], gated[:, 1, j * P:(j + 1) * P], ident[:, :])
                last.then_inc(y_ps, 1)

        @block.scalar
        def _(act):
            act.dma_start(half(ctx_sb, 0), ctx_in[0:BH, :, :].rearrange("b p d -> p b d")).then_inc(ctx_ld[0], 16)
            act.dma_start(key_words[:, :], key_row).then_inc(key_row_in, 16)
            act.dma_start(half(ctx_sb, 1), ctx_in[BH:B, :, :].rearrange("b p d -> p b d")).then_inc(ctx_ld[1], 16)

            def evacuate(dst, ps, full, done):
                act.wait_ge(full[0], full[1])
                nc.scalar.activation(dst, ps, ACT.Copy).then_inc(done, 1)

            act.wait_ge(warm_ready, 1)
            nc.scalar.activation(warm[:, 1:2], warm[:, 0:1], ACT.Exp)
            act.wait_ge(key_row_in, 16)
            nc.scalar.activation(neg_row[:, :], key_words[:, :].bitcast(U8), ACT.Copy, bias=MASK_NEG,
                                 scale=-MASK_NEG).then_inc(neg_ready, 1)

            def context_evacuated(h):
                evacuate(some(ctxT, range(h * BH, (h + 1) * BH)), ps_ctxT[h][:, :], (ctxT_ps, h + 1), ctxT_ready)

            def scores_operand(part):
                evacuate(some(xcT, PARTS[part]), columns(ps_xcT[part], PARTS[part]), (xcT_ps, part + 1), xcT_ready)

            def exponentials(part):
                act.wait_ge(neg_max_ready, part + 1)
                for j, b in enumerate(PARTS[part]):
                    last = nc.scalar.activation(probs[:, b, :], ps_scores[part][:, j * P:(j + 1) * P], ACT.Exp,
                                                bias=neg_max[:, b:b + 1], scale=exp_scale[:, b:b + 1], accum_out=denom[:, b:b + 1])
                last.then_inc(probs_ready, 1)

            def probs_evacuated(part):
                evacuate(some(probsT, PARTS[part]), columns(ps_probsT[part], PARTS[part]), (probsT_ps, part + 1), probsT_ready)

            def weights_rounded(hi, slot, cols):
                act.wait_ge(w_in[slot], 16)
                nc.scalar.activation(hi[slot][:, :], raw[slot][:, cols], ACT.Copy).then_inc(hi_rounded, 1)

            def tokens_rounded(part):
                evacuate(tokens(tok_hi, PARTS[part]), columns(ps_tokT[part], PARTS[part]), (tokT_ps, part + 1), tok_hi_ready)

            context_evacuated(0)
            scores_operand(0)
            scores_operand(1)
            act.wait_ge(small_in, 16)
            nc.scalar.activation(g_tanh[:, :], g_raw, ACT.Tanh).then_inc(g_ready, 1)
            exponentials(0)
            context_evacuated(1)
            probs_evacuated(0)
            exponentials(1)
            probs_evacuated(1)
            scores_operand(2)
            weights_rounded(pj_hi, 1, slice(HID, 2 * HID))
            weights_rounded(fc_hi, 0, slice(0, HID))
            weights_rounded(pj_hi, 0, slice(HID, 2 * HID))
            exponentials(2)
            probs_evacuated(2)
            nc.scalar.activation(warm[:, 1:2], warm[:, 0:1], ACT.Gelu_apprx_tanh)

            def gelu(slot, c, g, r, rounds):
                act.wait_ge(fc_done, g + 1)
                at_least(act, pj_done, g - RING + 1)
                if rounds:
                    nc.scalar.activation(hid_hi[:, r, :], ps_h[c][:, :], ACT.Gelu_apprx_tanh, bias=bias[slot][:, c:c + 1])
                nc.scalar.activation(hid[:, r, :], ps_h[c][:, :], ACT.Gelu_apprx_tanh,
                                     bias=bias[slot][:, c:c + 1]).then_inc(gelu_done, 1)

            def gates_evacuated(h):
                evacuate(gatesT[:, h, :], ps_gatesT[h][0:BH * E, 0:P], (gatesT_ps, h + 1), gatesT_ready)

            def top_tanhs(h):
                act.wait_ge(top_ready, h + 1)
                cols = slice(h * BH, (h + 1) * BH)
                nc.scalar.activation(top_tanh[:, cols], top_diff[:, cols], ACT.Tanh, scale=0.5).then_inc(tanh_ready, 1)

            for g in range(PEELED):
                number = FIRST_UNITS[g // C][0]
                gelu((number + 1) % 2, g % C, g, g % RING, g < ACT_ROUNDS or g % 2 == 0)
                if g == 3:
                    top_tanhs(0)
                if g == 4:
                    tokens_rounded(2)
                if g == 7:
                    gates_evacuated(0)
                if g == 10:
                    top_tanhs(1)
                if g == 13:
                    gates_evacuated(1)

            def chunk(it, k):
                gelu(1 - k // OF_EXPERT, k % C, PAIR * it + (PEELED + k), k % RING, k % 2 == 0)

            def expert_chunks(it, last_k):
                for k in range(last_k):
                    chunk(it, k)

            with act.Fori(0, LOOPS) as it:
                expert_chunks(it, PAIR)
            expert_chunks(LOOPS, OF_EXPERT - 2)
            act.wait_ge(y_ps, 1)
            nc.scalar.activation(some(y, range(BH, B)), ps_m[1][:, :], ACT.Copy, scale=g_tanh[:, 1:2]).then_inc(sum_scaled, 1)
            chunk(LOOPS, OF_EXPERT - 2)
            act.wait_ge(fc_done, CHUNKS)
            for piece in PIECES:
                nc.scalar.activation(hid[:, (CHUNKS - 1) % RING, piece], ps_h[C - 1][:, piece], ACT.Gelu_apprx_tanh,
                                     bias=bias[1][:, C - 1:C]).then_inc(gelu_done, 1)

        @block.vector
        def _(dve):
            steps = [0]

            def chain(ins):
                steps[0] += 1
                ins.then_inc(dve_step, 1)
                dve.wait_ge(dve_step, steps[0])

            stats_groups = [0]

            def statistics(src, batches):
                for b in batches:
                    last = nc.vector.bn_stats(stats[:, b, :], src[:, b, :])
                last.then_inc(stats_ready, 1)

            def variance_of(batches, moments, var, ready):
                stats_groups[0] += 1
                dve.wait_ge(stats_ready, stats_groups[0])
                for b in batches:
                    last = nc.vector.bn_aggr(moments[:, b, :], stats[:, b, :])
                chain(last)
                cols = slice(batches.start, batches.stop)
                nc.vector.tensor_scalar(var[:, cols], moments[:, cols, 1], LN_EPS, None, ALU.add).then_inc(ready, 1)

            def centre(batches):
                cols = slice(batches.start, batches.stop)
                nc.vector.tensor_tensor(xc[:, cols, :], x_sb[:, cols, :],
                                        moments1[:, cols, 0:1].to_broadcast([P, len(batches), D]),
                                        ALU.subtract).then_inc(xc_ready, 1)

            def largest_score(part):
                batches = PARTS[part]
                cols = slice(batches.start, batches.stop)
                dve.wait_ge(scores_ps, part + 1)
                chain(nc.vector.reduce_max(smax[:, cols], columns(ps_scores[part], batches).rearrange("p (b k) -> p b k", k=S), AX_X))
                nc.vector.scalar_tensor_tensor(neg_max[:, cols], smax[:, cols], -1.0, exp_scale[:, cols],
                                               ALU.mult, ALU.mult).then_inc(neg_max_ready, 1)

            def row_scales(part):
                cols = slice(PARTS[part].start, PARTS[part].stop)
                dve.wait_ge(probs_ready, part + 1)
                chain(nc.vector.reciprocal(inv_denom[:, cols], denom[:, cols]))
                chain(nc.vector.tensor_tensor(row_scale[:, cols], inv_denom[:, cols], q_scale[:, cols], ALU.mult))

            def residual(part):
                dve.wait_ge(att_ps, part + 1)
                for j, b in enumerate(PARTS[part]):
                    last = nc.vector.scalar_tensor_tensor(x2[:, b, :], ps_att[part][:, j * P:(j + 1) * P],
                                                          row_scale[:, b:b + 1], x_sb[:, b, :], ALU.mult, ALU.add)
                last.then_inc(x2_ready, 1)

            def normalise(part):
                dve.wait_ge(rstd2_ready, part + 1)
                for b in PARTS[part]:
                    last = nc.vector.tensor_scalar(x2n[:, b, :], x2[:, b, :], moments2[:, b, 0:1], rstd[:, 1, b:b + 1],
                                                   ALU.subtract, ALU.mult)
                last.then_inc(x2n_ready, 1)

            def split_tokens(part):
                if part < 2:
                    dve.wait_ge(tokT_ps, part + 1)
                    nc.vector.tensor_copy(tokens(tok_hi, PARTS[part]), columns(ps_tokT[part], PARTS[part])).then_inc(tok_hi_ready, 1)
                dve.wait_ge(tok_hi_ready, part + 1)
                nc.vector.tensor_tensor(tokens(tok_lo, PARTS[part]), columns(ps_tokT[part], PARTS[part]),
                                        tokens(tok_hi, PARTS[part]).bitcast(F32), ALU.subtract).then_inc(tok_ready, 1)

            def statistics2(part):
                dve.wait_ge(x2_ready, part + 1)
                statistics(x2, PARTS[part])

            def variance2(part):
                variance_of(PARTS[part], moments2, var_eps[:, 1, :], var2_ready)

            nc.vector.memset(warm[:, :], 0.0).then_inc(warm_ready, 1)
            nc.vector.memset(ones_row[:, :], 1.0).then_inc(ones_ready, 1)
            dve.wait_ge(x_in[0], 16)
            statistics(x_sb, range(0, BH))
            variance_of(range(0, BH), moments1, var_eps[:, 0, :], var1_ready)
            centre(PARTS[0])
            centre(PARTS[1])
            dve.wait_ge(small_in, 16)
            nc.vector.tensor_copy(mask_f[:, :], masks_u8).then_inc(mask_f_ready, 1)
            dve.wait_ge(rstd1_ready, 1)
            chain(nc.vector.tensor_scalar(exp_scale[:, 0:BH], rstd[:, 0, 0:BH], SCALE, None, ALU.mult))
            dve.wait_ge(x_in[1], 16)
            statistics(x_sb, range(BH, B))
            largest_score(0)
            variance_of(range(BH, B), moments1, var_eps[:, 0, :], var1_ready)
            largest_score(1)
            centre(PARTS[2])
            dve.wait_ge(rstd1_ready, 2)
            chain(nc.vector.tensor_scalar(exp_scale[:, BH:B], rstd[:, 0, BH:B], SCALE, None, ALU.mult))
            dve.wait_ge(g_ready, 1)
            dve.wait_ge(mask_f_ready, 1)
            chain(nc.vector.tensor_scalar(q_scale[:, :], mask_f[:, 0:B], g_tanh[:, 0:1], None, ALU.mult))

            row_scales(0)
            residual(0)
            statistics2(0)
            variance2(0)
            row_scales(1)
            residual(1)
            largest_score(2)
            normalise(0)
            statistics2(1)
            variance2(1)
            split_tokens(0)
            chain(nc.vector.tensor_copy(wr_parts[:, 0:E], wr_raw))
            nc.vector.tensor_tensor(wr_parts[:, E:2 * E], wr_raw, wr_parts[:, 0:E].bitcast(F32), ALU.subtract).then_inc(wr_ready, 1)
            normalise(1)
            row_scales(2)
            split_tokens(1)
            residual(2)
            statistics2(2)

            def lower_part(g, casts, r):
                dve.wait_ge(gelu_done, g + 1)
                at_least(dve, pj_done, g - RING + 1)
                if casts is not None:
                    nc.vector.tensor_copy(hid_hi[:, r, :], hid[:, r, :]).then_inc(hi_cast, 1)
                    dve.wait_ge(hi_cast, casts + 1)
                nc.vector.tensor_tensor(hid_lo[:, r, :], hid[:, r, :], hid_hi[:, r, :].bitcast(F32),
                                        ALU.subtract).then_inc(lo_done, 1)

            def gate_unit(slot, h, u, bank, loads, loaded=None):
                dve.wait_ge(pj_done, 4 * u + 4)
                if loads is not None:
                    dve.wait_ge(loaded or gate_in[slot], loads)
                at_least(dve, acc_added, u)
                nc.vector.scalar_tensor_tensor(gated[:, bank, :], ps_o[bank][:, :], bias[slot][:, C:C + 1],
                                               gate_bc[slot][:, h * N:(h + 1) * N], ALU.add, ALU.mult).then_inc(gated_done, 1)

            def top_two(h):
                cols = slice(h * BH, (h + 1) * BH)
                dve.wait_ge(logits_ps, h + 1)
                chain(nc.vector.tensor_copy(half(logits_sb, h), ps_logits[h][:, :, 0:E]))
                chain(nc.vector.tensor_tensor(half(logits_sb, h), half(logits_sb, h), ps_logits[h][:, :, E:2 * E], ALU.add))
                for b in range(h * BH, (h + 1) * BH):
                    last = nc.vector.max(top[:, b, :], logits_sb[:, b, :])
                chain(last)
                nc.vector.tensor_tensor(top_diff[:, cols], top[:, cols, 0], top[:, cols, 1], ALU.subtract).then_inc(top_ready, 1)
                for b in range(h * BH, (h + 1) * BH):
                    last = nc.vector.max_index(top_idx[:, b, :], top[:, b, :], logits_sb[:, b, :])
                chain(last)
                chain(nc.vector.tensor_copy(top_idx_f[:, :, cols], top_idx[:, cols, 0:2].rearrange("p b k -> p k b")))
                nc.vector.tensor_tensor(picks[:, :, cols, :], experts_of(expert_id[:, :].rearrange("p (k b e) -> p k b e", k=1, b=1)),
                                        experts_of(top_idx_f[:, :, cols].rearrange("p k (b e) -> p k b e", e=1)), ALU.is_equal).then_inc(index_ready, 1)

            dve.wait_ge(consts_ready, 1)
            for g in range(PEELED):
                lower_part(g, (g - ACT_ROUNDS) // 2 if g % 2 and g >= ACT_ROUNDS else None, g % RING)
                if g == 0:
                    variance2(2)
                if g == 2:
                    top_two(0)
                if g == 4:
                    split_tokens(2)
                if g == 7:
                    gate_unit(1, 0, 0, 0, None)
                if g == 9:
                    top_two(1)
                if g == 12:
                    gate_unit(0, 0, 1, 1, 16, loaded=gate_first)
                if g == 14:
                    gate_unit(1, 1, 2, 0, None)

            def chunk(it, k):
                lower_part(PAIR * it + (PEELED + k), PAIR // 2 * it + (PEELED + k - ACT_ROUNDS) // 2 if k % 2 else None, k % RING)

            def complete_unit(it, k):
                j = k - (C + 2)
                slot, h = (1 - j // OF_EXPERT, j // C % HALVES) if j >= 0 else (0, 1)
                loads = 16 * it + (32 if j >= 0 and slot == 0 else 16)
                gate_unit(slot, h, 4 * it + (4 + j // C), h, loads)

            def result(n, ps, base, batches):
                dve.wait_ge(y_ps, n)
                nc.vector.scalar_tensor_tensor(some(y, batches), ps, g_tanh[:, 1:2], some(base, batches),
                                               ALU.mult, ALU.add).then_inc(y_ready, 1)

            with dve.Fori(0, LOOPS) as it:
                for k in range(PAIR):
                    chunk(it, k)
                    if k % C == 2:
                        complete_unit(it, k)
            for k in range(OF_EXPERT - 2):
                chunk(LOOPS, k)
                if k == 2:
                    complete_unit(LOOPS, k)
            complete_unit(LOOPS, OF_EXPERT - 2)
            chunk(LOOPS, OF_EXPERT - 2)
            r = (CHUNKS - 1) % RING
            for n, piece in enumerate(PIECES):
                dve.wait_ge(gelu_done, CHUNKS + n)
                dve.wait_ge(pj_done, CHUNKS - RING)
                nc.vector.tensor_copy(hid_hi[:, r, piece], hid[:, r, piece]).then_inc(hi_cast, 1)
                dve.wait_ge(hi_cast, (CHUNKS - ACT_ROUNDS) // 2 + n)
                nc.vector.tensor_tensor(hid_lo[:, r, piece], hid[:, r, piece], hid_hi[:, r, piece].bitcast(F32),
                                        ALU.subtract).then_inc(lo_done, 1)

            def gate_piece(n):
                piece = PIECES[n]
                dve.wait_ge(last_done, n + 1)
                nc.vector.scalar_tensor_tensor(gated[:, 1, piece], ps_o[1 - n][:, piece], bias[1][:, C:C + 1],
                                               gate_bc[1][:, N + piece.start:N + piece.stop],
                                               ALU.add, ALU.mult).then_inc(gated_done, 1)

            dve.wait_ge(acc_added, UNITS - 1)
            gate_piece(0)
            result(2, ps_m[0][:, :], x2, range(0, BH))
            gate_piece(1)
            dve.wait_ge(y_part_ready, 1)
            for n, piece in enumerate(PIECES):
                result(3 + n, ps_h[n][:, piece], y, range(BH + piece.start // P, BH + piece.stop // P))

        @block.gpsimd
        def _(pool):
            nc.gpsimd.memset(ident[:, :], 0.0).then_inc(ident_zero, 1)
            pool.wait_ge(ident_zero, 1)
            nc.gpsimd.affine_select(out=ident[:, :], in_=ident[:, :], compare_op=ALU.not_equal, fill=1.0,
                                    base=0, pattern=[[-1, P]], channel_multiplier=1).then_inc(ident_ready, 1)
            nc.gpsimd.memset(minus_half[:, :], -0.5).then_inc(ident_zero, 1)
            pool.wait_ge(ident_zero, 2)

            for h in range(HALVES):
                last = nc.gpsimd.memset(acc[:, h, :], 0.0)
            last.then_inc(acc_added, 1)
            nc.gpsimd.memset(gate_bc[1][:, :], 1.0)
            for e in range(E):
                last = nc.gpsimd.memset(expert_id[:, e:e + 1], float(e))
            last.then_inc(consts_ready, 1)

            steps = [0]

            def chain(ins):
                steps[0] += 1
                ins.then_inc(pool_step, 1)
                pool.wait_ge(pool_step, steps[0])

            def inverse_std(k, batches, var_ready, count, ready):
                cols = slice(batches.start, batches.stop)
                pool.wait_ge(var_ready, count)
                return nc.gpsimd.tensor_tensor(rstd[:, k, cols], var_eps[:, k, cols], minus_half[:, 0:len(batches)],
                                               ALU.pow).then_inc(ready, 1)

            def masked_values(h):
                cols = slice(h * BH, (h + 1) * BH)
                pool.wait_ge(mask_f_ready, 1)
                pool.wait_ge(ctx_ld[h], 16)
                nc.gpsimd.tensor_tensor(v_masked[:, cols, :], ctx_sb[:, cols, :],
                                        mask_f[:, B + h * BH:B + (h + 1) * BH].rearrange("p (b o) -> p b o", o=1).to_broadcast([P, BH, D]),
                                        ALU.mult).then_inc(v_ready, 1)

            def split(hi, lo, src, number, rounded):
                if rounded:
                    pool.wait_ge(hi_rounded, rounded)
                else:
                    nc.gpsimd.tensor_scalar(hi[:, :], src, 1.0, 1.0, ALU.mult, ALU.mult).then_inc(hi_split, 1)
                    pool.wait_ge(hi_split, number)
                return nc.gpsimd.tensor_tensor(lo[:, :], src, hi[:, :].bitcast(F32), ALU.subtract)

            def split_fc(slot, loads, n, rounded=0):
                pool.wait_ge(w_in[slot], loads)
                nc.gpsimd.tensor_copy(bias[slot][:, 0:C], biasT[:, bass.ds((C + 1) * n, C)])
                number = 2 * n - 2 if not isinstance(n, int) or n else 1
                split(fc_hi[slot], fc_lo[slot], raw[slot][:, 0:HID], number, rounded).then_inc(fc_ready, 1)

            def split_pj(slot, n, rounded=0):
                nc.gpsimd.tensor_copy(bias[slot][:, C:C + 1], biasT[:, bass.ds((C + 1) * n + C, 1)])
                split(pj_hi[slot], pj_lo[slot], raw[slot][:, HID:2 * HID], 2 * n - 1, rounded).then_inc(pj_ready, 1)

            def add_unit(h, u, bank):
                pool.wait_ge(gated_done, u + 1)
                pool.wait_ge(acc_added, u + 1)
                nc.gpsimd.tensor_tensor(acc[:, h, :], acc[:, h, :], gated[:, bank, :], ALU.add).then_inc(acc_added, 1)

            def normalise(part):
                batches = PARTS[part]
                cols = slice(batches.start, batches.stop)
                inverse_std(1, batches, var2_ready, part + 1, rstd2_ready)
                chain(nc.gpsimd.tensor_scalar(minus_mean[:, :], moments2[:, cols, 0], -1.0, 1.0, ALU.mult, ALU.mult))
                pool.wait_ge(rstd2_ready, part + 1)
                for j, b in enumerate(batches):
                    last = nc.gpsimd.tensor_scalar(x2n[:, b, :], x2[:, b, :], minus_mean[:, j:j + 1], rstd[:, 1, b:b + 1],
                                                   ALU.add, ALU.mult)
                last.then_inc(x2n_ready, 1)

            def route(h):
                cols = slice(h * BH, (h + 1) * BH)
                pool.wait_ge(tanh_ready, h + 1)
                pool.wait_ge(index_ready, h + 1)
                nc.gpsimd.tensor_scalar(gate_top[:, 0, cols], top_tanh[:, cols], 0.5, 0.5, ALU.mult, ALU.add)
                chain(nc.gpsimd.tensor_scalar(gate_top[:, 1, cols], top_tanh[:, cols], -0.5, 0.5, ALU.mult, ALU.add))
                pick = picks[:, :, cols, :]
                chain(nc.gpsimd.tensor_tensor(pick, pick, experts_of(gate_top[:, :, cols].rearrange("p k (b e) -> p k b e", e=1)), ALU.mult))
                nc.gpsimd.tensor_tensor(half(gates, h), picks[:, 0, cols, :], picks[:, 1, cols, :], ALU.add).then_inc(gates_ready, 1)

            inverse_std(0, range(0, BH), var1_ready, 1, rstd1_ready)
            masked_values(0)
            inverse_std(0, range(BH, B), var1_ready, 2, rstd1_ready)
            pool.wait_ge(small_in, 16)
            split_fc(1, 16, 0)
            masked_values(1)
            inverse_std(1, PARTS[0], var2_ready, 1, rstd2_ready)
            split_pj(1, 0, rounded=1)
            inverse_std(1, PARTS[1], var2_ready, 2, rstd2_ready)
            split_fc(0, 16, 1, rounded=2)
            split_pj(0, 1, rounded=3)
            normalise(2)
            route(0)
            add_unit(0, 0, 0)
            route(1)
            pool.wait_ge(fc_done, 3 * C)
            pool.wait_ge(gelu_done, 3 * C)
            split_fc(1, 32, 2)
            add_unit(0, 1, 1)
            add_unit(1, 2, 0)
            pool.wait_ge(pj_done, 3 * C)
            split_pj(1, 2)
            pool.wait_ge(fc_done, 4 * C)
            pool.wait_ge(gelu_done, 4 * C)
            split_fc(0, 32, 3)
            add_unit(1, 3, 1)
            pool.wait_ge(pj_done, 4 * C)
            split_pj(0, 3)

            def expert_pair(it, last):
                add_unit(0, 4 * it + 4, 0)
                pool.wait_ge(fc_done, PAIR * it + (PEELED + OF_EXPERT))
                pool.wait_ge(gelu_done, PAIR * it + (PEELED + OF_EXPERT))
                split_fc(1, 16 * it + 48, 2 * it + 4)
                add_unit(1, 4 * it + 5, 1)
                pool.wait_ge(pj_done, PAIR * it + (PEELED + OF_EXPERT))
                split_pj(1, 2 * it + 4)
                add_unit(0, 4 * it + 6, 0)
                if not last:
                    pool.wait_ge(fc_done, PAIR * it + (PEELED + PAIR))
                    pool.wait_ge(gelu_done, PAIR * it + (PEELED + PAIR))
                    split_fc(0, 16 * it + 48, 2 * it + 5)
                add_unit(1, 4 * it + 7, 1)
                if not last:
                    pool.wait_ge(pj_done, PAIR * it + (PEELED + PAIR))
                    split_pj(0, 2 * it + 5)

            with pool.Fori(0, LOOPS - 1) as it:
                expert_pair(it, False)
            expert_pair(LOOPS - 1, True)
            pool.wait_ge(sum_scaled, 1)
            nc.gpsimd.tensor_tensor(half(y, 1), half(y, 1), half(x2, 1), ALU.add).then_inc(y_part_ready, 1)
            add_unit(0, UNITS - 2, 0)


def kernel(x, ctx_1024, mask_BxS2_bk1, mask_BxS2_bk0, g_xattn, g_ffn, L0_ffn_Wfc_s, L0_ffn_bfc_s, L0_ffn_Wproj_s,
           L0_ffn_bproj_s, L0_ffn_Wr, L0_ffn_Wfc, L0_ffn_bfc, L0_ffn_Wproj, L0_ffn_bproj):
    import numpy as np
    import concourse.bacc as bacc
    from concourse.bass_utils import run_bass_kernel_spmd

    P = 128
    q_mask, k_mask = np.asarray(mask_BxS2_bk1), np.asarray(mask_BxS2_bk0)
    w_fc = np.concatenate([np.asarray(L0_ffn_Wfc_s)[None], np.asarray(L0_ffn_Wfc)])
    w_pj = np.concatenate([np.asarray(L0_ffn_Wproj_s)[None], np.asarray(L0_ffn_Wproj)])
    b_fc = np.concatenate([np.asarray(L0_ffn_bfc_s)[None], np.asarray(L0_ffn_bfc)])
    b_pj = np.concatenate([np.asarray(L0_ffn_bproj_s)[None], np.asarray(L0_ffn_bproj)])
    n, hid, d = w_pj.shape
    w_pj = w_pj.reshape(n, hid // P, P, d).transpose(0, 2, 1, 3).reshape(n, P, hid)
    bias_cols = np.concatenate([b_fc.reshape(n, hid // P, P), b_pj[:, None, :]], axis=1).transpose(2, 0, 1)
    words = np.uint32
    per_partition = np.concatenate([
        np.ascontiguousarray(np.concatenate([q_mask, k_mask]).T).view(words),
        np.ascontiguousarray(bias_cols).reshape(P, -1).view(words),
        np.ascontiguousarray(L0_ffn_Wr).view(words),
        np.tile(np.concatenate([np.asarray(g_xattn), np.asarray(g_ffn)]), (P, 1)).view(words),
    ], axis=1)
    arrays = {
        "x": np.ascontiguousarray(x),
        "ctx_in": np.ascontiguousarray(ctx_1024),
        "key_row": np.ascontiguousarray(k_mask).reshape(1, -1).view(words),
        "per_partition": per_partition,
        "w_all": np.ascontiguousarray(np.concatenate([w_fc, w_pj], axis=2)),
    }
    nc = bacc.Bacc("TRN2", target_bir_lowering=False, num_devices=1)
    args = [nc.dram_tensor(f"in_{name}", a.shape, mybir.dt.from_np(a.dtype), kind="ExternalInput").ap()
            for name, a in arrays.items()]
    out = nc.dram_tensor("out_0", arrays["x"].shape, F32, kind="ExternalOutput").ap()
    flamingo_gated_moe(nc, *args, out)
    r = run_bass_kernel_spmd(nc, [{f"in_{name}": a for name, a in arrays.items()}], core_ids=[0])
    return r.results[0]["out_0"]
```
